# Optimizing a Trainium2 kernel written in Bass

```python
import numpy as np
import jax
import jax.numpy as jnp

def _softmax(x, axis=-1):
    return jax.nn.softmax(x, axis=axis)

def _gelu(x):
    return jax.nn.gelu(x, approximate=True)

def _silu(x):
    return jax.nn.silu(x)

def _sigmoid(x):
    return jax.nn.sigmoid(x)

def _layernorm(x, axis=-1, eps=1e-05):
    m = jnp.mean(x, axis=axis, keepdims=True)
    v = jnp.var(x, axis=axis, keepdims=True)
    return (x - m) / jnp.sqrt(v + eps)

def _scatter_add(tgt, idx, src, axis=0):
    return tgt.at[idx].add(src)

def _segment_sum(src, seg, n):
    return jax.ops.segment_sum(src, seg, n)
kernel_name = 'mk_sandwich_d1_jaxref_r4_6e304d'

def setup_inputs(seed: int=0):
    np.random.seed(seed)
    _w = jnp.asarray

    def _L0_attn_setup():
        import jax, jax.numpy as jnp
        import numpy as np
        BATCH, SEQ = (1, 512)
        D_MODEL, D_INNER, D_STATE, D_CONV = (256, 512, 16, 4)

        def _rms_norm(x, w, eps=1e-06):
            return x * jax.lax.rsqrt(jnp.mean(x * x, axis=-1, keepdims=True) + eps) * w
        key = jax.random.key(seed)
        ks = jax.random.split(key, 6)
        s = 0.02
        x = jax.random.normal(ks[0], (BATCH, SEQ, D_MODEL), jnp.float32)
        norm_w = jnp.ones((D_MODEL,), jnp.float32)
        in_proj_w = jax.random.normal(ks[1], (D_MODEL, 2 * D_INNER), jnp.float32) * s
        conv_w = jax.random.normal(ks[2], (D_INNER, 1, D_CONV), jnp.float32) * 0.2
        conv_b = jnp.zeros((D_INNER,), jnp.float32)
        A_log = jnp.tile(jnp.log(jnp.arange(1, D_STATE + 1, dtype=jnp.float32))[None, :], (D_INNER, 1))
        D = jnp.ones((D_INNER,), jnp.float32)
        x_proj_w = jax.random.normal(ks[3], (D_INNER, 2 * D_STATE + 1), jnp.float32) * s
        dt_proj_w = jax.random.normal(ks[4], (1, D_INNER), jnp.float32)
        dt_proj_b = jnp.full((D_INNER,), -4.0, jnp.float32)
        out_proj_w = jax.random.normal(ks[5], (D_INNER, D_MODEL), jnp.float32) * s
        return dict(x=x, norm_w=norm_w, in_proj_w=in_proj_w, conv_w=conv_w, conv_b=conv_b, A_log=A_log, D=D, x_proj_w=x_proj_w, dt_proj_w=dt_proj_w, dt_proj_b=dt_proj_b, out_proj_w=out_proj_w)
    _L0_attn_in = _L0_attn_setup()

    def _L0_ffn_setup():
        import jax, jax.numpy as jnp
        import numpy as np
        TOP_K = 4
        N_GROUP = 4
        TOPK_GROUP = 2
        ROUTED_SCALING = 1.0

        def _route(x_flat, gate_weight, e_bias):
            T = x_flat.shape[0]
            E = gate_weight.shape[0]
            logits = jnp.einsum('th,eh->te', x_flat, gate_weight)
            scores = jax.nn.sigmoid(logits)
            scores_for_choice = scores + e_bias[None, :]
            grp = scores_for_choice.reshape(T, N_GROUP, E // N_GROUP)
            top2, _ = jax.lax.top_k(grp, 2)
            group_scores = top2.sum(axis=-1)
            _, group_idx = jax.lax.top_k(group_scores, TOPK_GROUP)
            group_mask = jax.nn.one_hot(group_idx, N_GROUP, dtype=scores.dtype).sum(axis=1)
            score_mask = jnp.repeat(group_mask, E // N_GROUP, axis=1)
            tmp_scores = jnp.where(score_mask > 0, scores_for_choice, 0.0)
            _, topk_idx = jax.lax.top_k(tmp_scores, TOP_K)
            topk_weight = jnp.take_along_axis(scores, topk_idx, axis=1)
            denom = topk_weight.sum(axis=-1, keepdims=True) + 1e-20
            topk_weight = topk_weight / denom * ROUTED_SCALING
            return (topk_idx, topk_weight)
        key = jax.random.key(seed)
        k1, k2, k3, k4, k5 = jax.random.split(key, 5)
        B, S, H, I, E = (1, 512, 256, 128, 16)
        hidden_states = jax.random.normal(k1, (B, S, H), dtype=jnp.float32)
        gate_weight = jax.random.normal(k2, (E, H), dtype=jnp.float32) * (1.0 / np.sqrt(H))
        e_bias = jnp.zeros((E,), dtype=jnp.float32)
        gate_proj = jax.random.normal(k3, (E, I, H), dtype=jnp.float32) * 0.02
        up_proj = jax.random.normal(k4, (E, I, H), dtype=jnp.float32) * 0.02
        down_proj = jax.random.normal(k5, (E, H, I), dtype=jnp.float32) * 0.02
        return {'hidden_states': hidden_states, 'gate_weight': gate_weight, 'e_bias': e_bias, 'gate_proj': gate_proj, 'up_proj': up_proj, 'down_proj': down_proj}
    _L0_ffn_in = _L0_ffn_setup()
    _d = {'L0_attn_x': _L0_attn_in['x'], 'L0_attn_norm_w': _L0_attn_in['norm_w'], 'L0_attn_in_proj_w': _L0_attn_in['in_proj_w'], 'L0_attn_conv_w': _L0_attn_in['conv_w'], 'L0_attn_conv_b': _L0_attn_in['conv_b'], 'L0_attn_A_log': _L0_attn_in['A_log'], 'L0_attn_D': _L0_attn_in['D'], 'L0_attn_x_proj_w': _L0_attn_in['x_proj_w'], 'L0_attn_dt_proj_w': _L0_attn_in['dt_proj_w'], 'L0_attn_dt_proj_b': _L0_attn_in['dt_proj_b'], 'L0_attn_out_proj_w': _L0_attn_in['out_proj_w'], 'L0_ffn_gate_weight': _L0_ffn_in['gate_weight'], 'L0_ffn_e_bias': _L0_ffn_in['e_bias'], 'L0_ffn_gate_proj': _L0_ffn_in['gate_proj'], 'L0_ffn_up_proj': _L0_ffn_in['up_proj'], 'L0_ffn_down_proj': _L0_ffn_in['down_proj']}
    _x0 = _d['L0_attn_x']
    _d['L0_attn_x'] = jax.random.normal(jax.random.fold_in(jax.random.key(seed), 1), (8, 1024, 256), dtype=_x0.dtype)
    del _x0
    return _d

def reference(L0_attn_x, L0_attn_norm_w, L0_attn_in_proj_w, L0_attn_conv_w, L0_attn_conv_b, L0_attn_A_log, L0_attn_D, L0_attn_x_proj_w, L0_attn_dt_proj_w, L0_attn_dt_proj_b, L0_attn_out_proj_w, L0_ffn_gate_weight, L0_ffn_e_bias, L0_ffn_gate_proj, L0_ffn_up_proj, L0_ffn_down_proj):

    def _L0_attn_ref(x, norm_w, in_proj_w, conv_w, conv_b, A_log, D, x_proj_w, dt_proj_w, dt_proj_b, out_proj_w):
        import jax, jax.numpy as jnp
        import numpy as np
        BATCH, SEQ = (1, 512)
        D_MODEL, D_INNER, D_STATE, D_CONV = (256, 512, 16, 4)

        def _rms_norm(x, w, eps=1e-06):
            return x * jax.lax.rsqrt(jnp.mean(x * x, axis=-1, keepdims=True) + eps) * w
        residual = x
        xn = _rms_norm(x, norm_w)
        xz = xn @ in_proj_w
        xb, z = jnp.split(xz, 2, axis=-1)
        xc = jnp.transpose(xb, (0, 2, 1))
        xc = jnp.pad(xc, ((0, 0), (0, 0), (D_CONV - 1, 0)))
        xc = jax.lax.conv_general_dilated(xc, conv_w, window_strides=(1,), padding='VALID', feature_group_count=D_INNER, dimension_numbers=('NCH', 'OIH', 'NCH')) + conv_b[None, :, None]
        xc = jax.nn.silu(jnp.transpose(xc, (0, 2, 1)))
        A = -jnp.exp(A_log)
        x_dbl = xc @ x_proj_w
        dt, Bm, Cm = jnp.split(x_dbl, [1, 1 + D_STATE], axis=-1)
        dt = jax.nn.softplus(dt @ dt_proj_w + dt_proj_b)
        dA = jnp.exp(dt[..., None] * A[None, None])
        dBx = dt[..., None] * Bm[:, :, None, :] * xc[..., None]

        def step(h, inp):
            dA_t, dBx_t, C_t = inp
            h = dA_t * h + dBx_t
            y_t = jnp.einsum('bds,bs->bd', h, C_t)
            return (h, y_t)
        h0 = jnp.zeros((x.shape[0], D_INNER, D_STATE), x.dtype)
        _, ys = jax.lax.scan(step, h0, (jnp.swapaxes(dA, 0, 1), jnp.swapaxes(dBx, 0, 1), jnp.swapaxes(Cm, 0, 1)))
        y = jnp.swapaxes(ys, 0, 1)
        y = y + xc * D[None, None, :]
        y = y * jax.nn.silu(z)
        y = y @ out_proj_w
        return y + residual

    def _L0_ffn_ref(hidden_states, gate_weight, e_bias, gate_proj, up_proj, down_proj):
        import jax, jax.numpy as jnp
        import numpy as np
        TOP_K = 4
        N_GROUP = 4
        TOPK_GROUP = 2
        ROUTED_SCALING = 1.0

        def _route(x_flat, gate_weight, e_bias):
            T = x_flat.shape[0]
            E = gate_weight.shape[0]
            logits = jnp.einsum('th,eh->te', x_flat, gate_weight)
            scores = jax.nn.sigmoid(logits)
            scores_for_choice = scores + e_bias[None, :]
            grp = scores_for_choice.reshape(T, N_GROUP, E // N_GROUP)
            top2, _ = jax.lax.top_k(grp, 2)
            group_scores = top2.sum(axis=-1)
            _, group_idx = jax.lax.top_k(group_scores, TOPK_GROUP)
            group_mask = jax.nn.one_hot(group_idx, N_GROUP, dtype=scores.dtype).sum(axis=1)
            score_mask = jnp.repeat(group_mask, E // N_GROUP, axis=1)
            tmp_scores = jnp.where(score_mask > 0, scores_for_choice, 0.0)
            _, topk_idx = jax.lax.top_k(tmp_scores, TOP_K)
            topk_weight = jnp.take_along_axis(scores, topk_idx, axis=1)
            denom = topk_weight.sum(axis=-1, keepdims=True) + 1e-20
            topk_weight = topk_weight / denom * ROUTED_SCALING
            return (topk_idx, topk_weight)
        B, S, H = hidden_states.shape
        E = gate_proj.shape[0]
        x = hidden_states.reshape(-1, H).astype(jnp.float32)
        topk_idx, topk_weight = _route(x, gate_weight, e_bias)
        combine = (jax.nn.one_hot(topk_idx, E, dtype=x.dtype) * topk_weight[..., None]).sum(axis=1)
        g = jnp.einsum('th,eih->tei', x, gate_proj)
        u = jnp.einsum('th,eih->tei', x, up_proj)
        act = jax.nn.silu(g) * u
        expert_out = jnp.einsum('tei,ehi->teh', act, down_proj)
        y = jnp.einsum('teh,te->th', expert_out, combine)
        return y.reshape(B, S, H)
    x = L0_attn_x
    x = x + _layernorm(_L0_attn_ref(_layernorm(x, axis=-1), L0_attn_norm_w, L0_attn_in_proj_w, L0_attn_conv_w, L0_attn_conv_b, L0_attn_A_log, L0_attn_D, L0_attn_x_proj_w, L0_attn_dt_proj_w, L0_attn_dt_proj_b, L0_attn_out_proj_w), axis=-1)
    x = x + _layernorm(_L0_ffn_ref(_layernorm(x, axis=-1), L0_ffn_gate_weight, L0_ffn_e_bias, L0_ffn_gate_proj, L0_ffn_up_proj, L0_ffn_down_proj), axis=-1)
    return x

_drawn_inputs = setup_inputs


def setup_inputs(seed=0):
    import zlib

    import numpy as np

    out = dict(_drawn_inputs(seed))
    spreads = {'L0_attn_norm_w': (1.0, 0.6),
     'L0_attn_conv_b': (0.0, 0.372),
     'L0_attn_D': (1.0, 0.6),
     'L0_attn_dt_proj_b': (-4.0, 0.6),
     'L0_ffn_e_bias': (0.0, 0.1)}
    factors = {'L0_attn_conv_w': 2.785,
     'L0_attn_A_log': 8.0,
     'L0_attn_x_proj_w': 8.0,
     'L0_attn_dt_proj_w': 8.0}
    for name, (base, spread) in spreads.items():
        noise = np.random.default_rng([zlib.crc32(name.encode()), seed]).standard_normal(out[name].shape)
        drawn = base * np.exp(spread * noise) if base else spread * noise
        out[name] = jnp.asarray(drawn.astype(out[name].dtype))
    for name, factor in factors.items():
        out[name] = (out[name] * factor).astype(out[name].dtype)
    return out
```

```python
from contextlib import ExitStack

import numpy as np
import concourse.bass as bass
from concourse import mybir

F32 = mybir.dt.float32
I32 = mybir.dt.int32
ALU = mybir.AluOpType
ACT = mybir.ActivationFunctionType
AX = mybir.AxisListType

P = 128
BATCH, SEQ, DM = 8, 1024, 256
DI, NS, TAPS = 512, 16, 4
NE, NG, DE, TOPK, TOPG = 16, 4, 128, 4, 2
CH = 256
TB = CH // P
KM = DM // P
MT = DI // P
NCH = SEQ // CH
NTILE = BATCH * MT
SG = 4
CB = P // SG
NSIG = NS // SG
NBETA = P // CB
UNITS = NSIG * NBETA
NA, NH = 2, 6
SLOT = [n if n < NH else (n - NH) % (NH - 1) for n in range(UNITS)]
PAIRS = NE // 2
STEPS = TB * PAIRS
HIST = TAPS - 1
LN_EPS, RMS_EPS = 1e-5, 1e-6
RSQRT_MAGIC = float(0x5F3759DF)

FIRST_F, FIRST_S, FIRST_Y, FIRST_P, FIRST_M, FIRST_Z = -NCH, 0, 1, NCH, NCH + 1, NCH + 2
PARTS = dict(F=FIRST_F, S=FIRST_S, Y=FIRST_Y, P=FIRST_P, M=FIRST_M, Z=FIRST_Z)


def segments():
    cuts = sorted({f for f in PARTS.values()} | {f + NTILE for f in PARTS.values()})
    out = []
    for a, b in zip(cuts, cuts[1:]):
        out.append((a, b, {p: f <= a < f + NTILE for p, f in PARTS.items()}))
    return out


def rsqrt_names(tag):
    return [f"{tag}_half", f"{tag}_guess"] + [f"{tag}_{s}{n}" for n in range(3) for s in ("a", "b", "y")]


TICK = {}


def settle(eng):
    if eng is TICK.get("engine"):
        eng.sem_inc(TICK["sem"], 1)


class Steps:

    def __init__(self, sem, names):
        self.sem, self.names, self.per, self.at = sem, names, len(names), 0
        assert len(set(names)) == len(names)

    def credit(self, eng):
        eng.sem_inc(self.sem, self.per)

    def done(self, ins, name):
        assert self.names[self.at % self.per] == name, (name, self.names[self.at % self.per])
        self.at += 1
        ins.then_inc(self.sem, 1)

    def wait(self, eng, it, name):
        eng.wait_ge(self.sem, it * self.per + (self.per + self.names.index(name) + 1))
        settle(eng)


def slot_before(n):
    m = n - 1
    while SLOT[m % UNITS] != SLOT[n]:
        m -= 1
    return m // UNITS, m % UNITS


class Moves:

    def __init__(self, sem, n=1):
        self.sem, self.per = sem, 16 * n

    def credit(self, eng):
        eng.sem_inc(self.sem, self.per)

    def add(self, ins):
        ins.then_inc(self.sem, 16)

    def wait(self, eng, it):
        eng.wait_ge(self.sem, it * self.per + 2 * self.per)
        settle(eng)


def sandwich_kernel(nc, x, w_in, w_out, w_gu, w_dn, w_x, w_rt, cols, alog, ebias, consts, sel_dt, keep, out):
    with ExitStack() as ctx:
        def sb(name, shape, dt=F32):
            return ctx.enter_context(nc.sbuf_tensor(name, shape, dt))

        def pb(name):
            return ctx.enter_context(nc.psum_tensor(name, [P, 512], F32))

        def sem(name):
            return ctx.enter_context(nc.semaphore(name))

        def scratch(name, shape):
            return nc.dram_tensor(name, shape, F32, kind="Internal").ap()

        dt_d = scratch("dt_d", (BATCH * DI, SEQ))
        dx_d = scratch("dx_d", (BATCH * DI, SEQ))
        xc_d = scratch("xc_d", (BATCH * DI, SEQ))
        sz_d = scratch("sz_d", (BATCH * DI, SEQ))
        y_d = scratch("y_d", (BATCH * DI, SEQ))
        bc_d = scratch("bc_d", (BATCH * 2 * NS, SEQ))
        xn_d = scratch("xn_d", (BATCH * SEQ, DM))
        x1_d = scratch("x1_d", (BATCH * SEQ, DM))

        def tokens(t, c):
            return t.rearrange("(c b p) h -> c p b h", b=TB, p=P)[c]

        def chunk(t, b, j):
            return t.rearrange("(b m p) (j t) -> b j p m t", m=MT, p=P, j=NCH)[b, j]

        def tile_of(t, i):
            return t.rearrange("(i p) t -> i p t", p=P)[i]

        Win = sb("Win", [P, KM, 2 * DI])
        Wout = sb("Wout", [P, MT, DM])
        Wgu = sb("Wgu", [P, KM, PAIRS, 4 * DE])
        Wdn = sb("Wdn", [P, NE, DM])
        Wx = sb("Wx", [P, MT, 2 * NS + 1])
        Wrt = sb("Wrt", [P, KM, NE])
        Cols = sb("Cols", [P, MT * (TAPS + 4) + KM])
        ADall = sb("ADall", [P, MT, UNITS + 1])
        Acur = sb("Acur", [P, UNITS])
        Ebias = sb("Ebias", [P, TB * NE])
        Cst = sb("Cst", [P, P + CB + NE * NE + NG * NG])
        SelDt = sb("SelDt", [2 * NS + 1, P])
        conv_w = Cols[:, 0:MT * TAPS].rearrange("p (m k) -> p m k", m=MT)
        conv_b, dt_w, dt_b, d_col = (Cols[:, MT * (TAPS + k):MT * (TAPS + k + 1)] for k in range(4))
        norm_w = Cols[:, MT * (TAPS + 4):MT * (TAPS + 4) + KM]
        ident = Cst[:, 0:P]
        sel_y = Cst[:, P:P + CB]
        before = Cst[:, P + CB:P + CB + NE * NE]
        before_g = Cst[:, P + CB + NE * NE:P + CB + NE * NE + NG * NG]

        fa = sb("fa", [P, 2 * TB * DM])
        xin = fa[:, 0:TB * DM].rearrange("p (b h) -> p b h", b=TB)
        xT = fa[:, TB * DM:].rearrange("p (q t) -> p q t", q=KM)
        low = fa[:, :].rearrange("p (m t) -> p m t", m=MT)
        xb = sb("xb", [P, MT, HIST + CH])
        xc = sb("xc", [P, MT, CH])
        sz = sb("sz", [P, MT, CH])
        xn = sz[:, 0:2, :]
        assert DM == CH and TB == 2
        dt = xb[:, :, HIST:HIST + CH]
        xd = sb("xd", [2 * NS + 1, CH])
        kp = sb("kp", [P, 1])
        f_st = sb("f_st", [P, TB, 6])
        f_mv = sb("f_mv", [P, TB, 2])
        f_w = sb("f_w", [P, 3, 2 * TB])
        mark = sb("mark", [P, 1])
        dtr = sb("dtr", [P, NBETA, SEQ])
        dxr = sb("dxr", [P, NBETA, SEQ])
        Bb = sb("Bb", [P, NSIG, SEQ])
        Cb = sb("Cb", [P, NSIG, SEQ])
        dA = sb("dA", [P, NA, SEQ])
        hs = sb("hs", [P, NH, SEQ])
        yt = sb("yt", [P, SEQ])
        gt = sb("gt", [P, SEQ])
        y2 = sb("y2", [P, MT, CH])
        rn = sb("rn", [P, TB, DM])
        x1 = sb("x1", [P, TB, DM])
        x2T = sb("x2T", [P, KM, CH])
        p_st = sb("p_st", [P, TB, 6])
        p_mv = sb("p_mv", [P, TB, 2])
        p_w = sb("p_w", [P, 3, TB])
        R = sb("R", [P, 12, TB * NE])
        assert MT * CH == 2 * TB * NE * NE
        RR = y2[:, :, :].rearrange("p (k m) t -> p k (m t)", k=2)
        comb = sb("comb", [P, TB * NE])
        x2m = sb("x2m", [P, KM, CH])
        cm = sb("cm", [P, TB * NE])
        th = sb("th", [P, 2, 2 * DE])
        aT = sb("aT", [P, 2, 2 * DE])
        my = sb("my", [P, TB, DM])
        x1m = sb("x1m", [P, TB, DM])
        z_st = sb("z_st", [P, TB, 6])
        z_mv = sb("z_mv", [P, TB, 2])
        z_w = sb("z_w", [P, 3, TB])

        Y = [pb("Y0"), pb("Y1")]
        GU = [pb("GU0"), pb("GU1")]
        TR, MY, FB, PBK = pb("TR"), pb("MY"), pb("FB"), pb("PBK")

        f_dve = Steps(sem("f_dve"), ["bn0", "bn1", "both", "ag0", "ag1", "w1", "w2"] + rsqrt_names("r")
                      + ["xn0", "xn1", "xr0", "xr1"] + [f"c{k}{m}" for k in range(TAPS) for m in range(MT)]
                      + ["hist", "near", "lost", "dt", "dx"])
        f_pool = Steps(sem("f_pool"), ["ln"])
        f_pe = Steps(sem("f_pe"), ["tr", "ip0", "ip1", "ip2", "ip3", "xp", "db"])
        f_act = Steps(sem("f_act"), ["xT", "e0", "e1", "e2", "e3", "silu_z", "silu_x", "xd"]
                      + [f"{k}{m}" for m in range(MT) for k in ("abs", "relu")] + ["exp", "ln"])
        s_act = Steps(sem("s_act"), ["ad"] + [f"dA{n}" for n in range(UNITS)])
        s_u = Steps(sem("s_u"), [f"u{n}" for n in range(UNITS)])
        s_sc = Steps(sem("s_sc"), [f"h{n}" for n in range(UNITS)])
        s_hc = Steps(sem("s_hc"), [f"c{n}" for n in range(UNITS)])
        s_pe = Steps(sem("s_pe"), [f"y{s}" for s in range(NSIG)])
        y_dve = Steps(sem("y_dve"), ["skip0", "skip1"])
        y_pool = Steps(sem("y_pool"), ["gate"])
        route = (["sfc", "hi", "lo", "t1", "t2a", "t2b", "t2", "gs", "ggt", "geq", "gq", "ga", "gr", "gm",
                  "tmp", "gt", "eq", "eqb", "ad", "rk", "w", "ws", "we", "wr", "comb"])
        p_dve = Steps(sem("p_dve"), ["r", "bn0", "bn1", "both", "ag0", "ag1", "w1"] + rsqrt_names("r") + ["o0", "o1", "x1"]
                      + ["Bbn0", "Bbn1", "Bboth", "Bag0", "Bag1", "Bw1"] + rsqrt_names("q") + ["x20", "x21"] + route)
        p_pe = Steps(sem("p_pe"), ["op", "tr", "rt"])
        p_act = Steps(sem("p_act"), ["x2T", "sig", "x2m", "cm"])
        m_pe_g = Steps(sem("m_pe_g"), [f"g{n}" for n in range(STEPS)])
        m_pe_t = Steps(sem("m_pe_t"), [f"t{n}" for n in range(STEPS)])
        m_pe_d = Steps(sem("m_pe_d"), [f"d{n}" for n in range(STEPS)])
        m_th = Steps(sem("m_th"), [f"th{n}" for n in range(STEPS)])
        m_aT = Steps(sem("m_aT"), [f"aT{n}" for n in range(STEPS)])
        m_my = Steps(sem("m_my"), [f"my{b}" for b in range(TB)])
        m_dve = Steps(sem("m_dve"), [s for n in range(STEPS) for s in (f"a{n}", f"e{n}", f"f{n}")])
        z_dve = Steps(sem("z_dve"), ["bn0", "bn1", "both", "ag0", "ag1", "w1"] + rsqrt_names("r") + ["o0", "o1", "out"])

        ld_w = sem("ld_w")
        w_act, w_dve = sem("w_act"), sem("w_dve")
        ld_xin = Moves(sem("ld_xin"), 2)
        ld_dt = [Moves(sem(f"ld_dt{b}"), 2) for b in range(NBETA)]
        ld_bc = [Moves(sem(f"ld_bc{s}"), 2) for s in range(NSIG)]
        ld_yt, ld_y2, ld_p, ld_x1 = Moves(sem("ld_yt"), 2), Moves(sem("ld_y2")), Moves(sem("ld_p"), 2), Moves(sem("ld_x1"))
        st_xn, st_sz, st_xc, st_xd, st_dt, st_dx = (Moves(sem(f"st_{k}")) for k in ("xn", "sz", "xc", "xd", "dt", "dx"))
        st_y, st_x1, st_out = (Moves(sem(f"st_{k}")) for k in ("y", "x1", "out"))

        block = ctx.enter_context(nc.Block())

        weights = [(Win, w_in), (Cols, cols), (Cst, consts), (Wx, w_x), (SelDt, sel_dt), (Wout, w_out), (Wrt, w_rt),
                   (Ebias, ebias), (Wgu, w_gu), (Wdn, w_dn)]

        @block.sync
        def _(sp):
            TICK.update(engine=sp, sem=sem("sp_tick"))
            for m in (ld_xin, *ld_dt, *ld_bc, ld_yt, ld_y2, ld_p, ld_x1,
                      st_xn, st_sz, st_xc, st_xd, st_dt, st_dx, st_y, st_x1, st_out):
                m.credit(sp)
            sp.dma_start(ADall[:, :, :], alog).then_inc(ld_w, 16)
            for t, src in weights:
                full = t[tuple(slice(None) for _ in src.shape)]
                sp.dma_start(full, src).then_inc(ld_w, 16)

            def load_tile(i):
                for beta in range(NBETA):
                    rows = slice(beta * CB, (beta + 1) * CB)
                    s_act.wait(sp, i - 1, f"dA{UNITS - NBETA + beta}")
                    ld_dt[beta].add(sp.dma_start(dtr[:, beta, :], tile_of(dt_d, i)[rows, :].partition_broadcast(SG)))
                    s_u.wait(sp, i - 1, f"u{UNITS - NBETA + beta}")
                    ld_dt[beta].add(sp.dma_start(dxr[:, beta, :], tile_of(dx_d, i)[rows, :].partition_broadcast(SG)))

            def load_bc(b):
                last = b * NCH - 1
                for s in range(NSIG):
                    end = (s + 1) * NBETA - 1
                    s_u.wait(sp, last, f"u{end}")
                    for k, (t, steps, name) in enumerate(((Bb, s_u, f"u{end}"), (Cb, s_hc, f"c{end}"))):
                        steps.wait(sp, last, name)
                        src = bc_d.rearrange("(b k s g) t -> b k s g t", b=BATCH, k=2, g=SG)[b, k, s]
                        ld_bc[s].add(sp.dma_start(t[:, s, :], src.unsqueeze(1).broadcast_to([SG, CB, SEQ])))

            def body(b, j, on):
                i = b * NCH + j
                cf, cp, cz = i - FIRST_F, i - FIRST_P, i - FIRST_Z
                if on["P"]:
                    p_dve.wait(sp, cp - 1, "comb")
                    st_x1.wait(sp, cp - 1)
                    ld_p.add(sp.dma_start(rn[:, :, :], tokens(xn_d, cp)))
                    ld_p.add(sp.dma_start(x1[:, :, :], tokens(x, cp)))
                if on["Z"]:
                    st_out.wait(sp, cz - 1)
                    st_x1.wait(sp, cz)
                    ld_x1.add(sp.dma_start(x1m[:, :, :], tokens(x1_d, cz)))
                if on["F"]:
                    f_dve.wait(sp, cf - 1, "dt")
                    ld_xin.add(sp.dma_start(xin[:, :, :], tokens(x, cf)))
                    ld_xin.add(sp.dma_start(kp[:, :], keep[j]))
                if on["Y"]:
                    y_pool.wait(sp, i - FIRST_Y, "gate")
                    st_y.add(sp.dma_start(tile_of(y_d, i - FIRST_Y), yt[:, :]))
                if on["S"]:
                    st_y.wait(sp, i - FIRST_Y)
                    y_pool.wait(sp, i - FIRST_Y, "gate")
                    ld_yt.add(sp.dma_start(yt[:, :], tile_of(xc_d, i)))
                    ld_yt.add(sp.dma_start(gt[:, :], tile_of(sz_d, i)))
                if on["P"]:
                    if on["Y"]:
                        st_y.wait(sp, i - FIRST_Y)
                    p_dve.wait(sp, cp - 1, "comb")
                    ld_y2.add(sp.dma_start(y2[:, :, :], chunk(y_d, b - 1, j)))
                if on["F"]:
                    f_dve.wait(sp, cf, "xn1")
                    st_xn.add(sp.dma_start(tokens(xn_d, cf), xn[:, :, :]))
                if on["Z"]:
                    z_dve.wait(sp, cz, "out")
                    st_out.add(sp.dma_start(tokens(out, cz), x1m[:, :, :]))
                if on["P"]:
                    p_dve.wait(sp, cp, "x1")
                    st_x1.add(sp.dma_start(tokens(x1_d, cp), x1[:, :, :]))
                if on["F"]:
                    f_act.wait(sp, cf, "silu_z")
                    st_sz.add(sp.dma_start(chunk(sz_d, b + 1, j), sz[:, :, :]))
                    f_act.wait(sp, cf, "silu_x")
                    st_xc.add(sp.dma_start(chunk(xc_d, b + 1, j), xc[:, :, :]))
                    f_act.wait(sp, cf, "xd")
                    st_xd.add(sp.dma_start(
                        bc_d.rearrange("(b r) (j t) -> b j r t", b=BATCH, j=NCH)[b + 1, j], xd[0:2 * NS, :]))
                    f_dve.wait(sp, cf, "dt")
                    st_dt.add(sp.dma_start(chunk(dt_d, b + 1, j), dt))
                    f_dve.wait(sp, cf, "dx")
                    st_dx.add(sp.dma_start(chunk(dx_d, b + 1, j), xc[:, :, :]))
                    for st in (st_sz, st_xc, st_xd, st_dt, st_dx):
                        st.wait(sp, cf)

            def whole(b, j0, j1, on, prefetch=True):
                def one(j):
                    body(b, j, on)
                    if prefetch:
                        load_tile(b * NCH + j + 1)
                if j1 - j0 == 1:
                    one(j0)
                else:
                    with sp.Fori(j0, j1) as j:
                        one(j)

            parts_at = lambda i: next(on for a, e, on in segments() if a <= i < e)
            segs = segments()

            def row(b):
                j = 0
                while j < NCH:
                    i = b * NCH + j
                    seg = next(((a, e, on) for a, e, on in segs if a <= i < e), None)
                    if seg is None:
                        return
                    a, e, on = seg
                    j1 = min(NCH, e - b * NCH)
                    if b == -1:
                        whole(b, j, j1, on, prefetch=False)
                    elif b == BATCH - 1:
                        if j1 == NCH:
                            if j1 - 1 > j:
                                whole(b, j, j1 - 1, on)
                            whole(b, j1 - 1, j1, on, prefetch=False)
                        else:
                            whole(b, j, j1, on)
                    elif b >= BATCH:
                        whole(b, j, j1, on, prefetch=False)
                    else:
                        whole(b, j, j1, on)
                    j = j1

            row(-1)
            load_tile(0)
            load_bc(0)
            row(0)
            load_bc(1)
            row(1)
            load_bc(2)
            all_parts = parts_at(2 * NCH)
            with sp.Fori(2, BATCH - 1) as b:
                with sp.Fori(0, NCH) as j:
                    body(b, j, all_parts)
                    load_tile(b * NCH + j + 1)
                load_bc(b + 1)
            row(BATCH - 1)
            row(BATCH)
            row(BATCH + 1)
            for st, n in ((st_xn, NTILE), (st_y, NTILE), (st_x1, NTILE), (st_out, NTILE)):
                st.wait(sp, n - 1)

        def run(eng, body):
            for a, e, on in segments():
                if e - a == 1:
                    body(a, on)
                else:
                    with eng.Fori(a - FIRST_F, e - FIRST_F) as k:
                        body(k, on, FIRST_F)

        @block.tensor
        def _(pe):
            for s in (f_pe, s_pe, p_pe, m_pe_g, m_pe_t, m_pe_d):
                s.credit(pe)
            pe.wait_ge(ld_w, 16 * (len(weights) + 1))
            pe.wait_ge(w_dve, 1)

            def body(k, on, base=0):
                i = k + base
                cf, cp, cm_ = i - FIRST_F, i - FIRST_P, i - FIRST_M

                def gate_up(n):
                    if n == 0:
                        p_act.wait(pe, cm_, "x2m")
                    g = GU[n % 2]
                    m_dve.wait(pe, cm_ if n >= 2 else cm_ - 1, f"f{(n - 2) % STEPS}")
                    b, p = divmod(n, PAIRS)
                    for q in range(KM):
                        mm = pe.matmul(g[:, :], x2m[:, q, b * P:(b + 1) * P], Wgu[:, q, p, :],
                                       start=(q == 0), stop=(q == KM - 1))
                    m_pe_g.done(mm, f"g{n}")

                def turn(n):
                    m_dve.wait(pe, cm_, f"f{n}")
                    m_aT.wait(pe, cm_ if n >= 1 else cm_ - 1, f"aT{(n - 1) % STEPS}")
                    for e in range(2):
                        mm = pe.transpose(TR[:, e * DE:(e + 1) * DE], th[:, n % 2, e * DE:(e + 1) * DE], ident)
                    m_pe_t.done(mm, f"t{n}")

                def down(n):
                    b, p = divmod(n, PAIRS)
                    m_aT.wait(pe, cm_, f"aT{n}")
                    if p == 0:
                        m_my.wait(pe, cm_ if b else cm_ - 1, f"my{(b - 1) % TB}")
                    for e in range(2):
                        mm = pe.matmul(MY[:, b * DM:(b + 1) * DM], aT[:, n % 2, e * DE:(e + 1) * DE],
                                       Wdn[:, 2 * p + e, :], start=(p == 0 and e == 0),
                                       stop=(p == PAIRS - 1 and e == 1))
                    m_pe_d.done(mm, f"d{n}")

                def add_states(s):
                    if s == 0:
                        y_dve.wait(pe, i - 1, "skip1")
                    s_hc.wait(pe, i, f"c{(s + 1) * NBETA - 1}")
                    for h in range(2):
                        for beta in range(NBETA):
                            mm = pe.matmul(Y[h][beta * CB:(beta + 1) * CB, :], sel_y,
                                           hs[:, SLOT[s * NBETA + beta], h * 512:(h + 1) * 512],
                                           start=(s == 0), stop=(s == NSIG - 1), tile_position=(0, beta * CB))
                    s_pe.done(mm, f"y{s}")

                def f_turn():
                    f_dve.wait(pe, cf, "xr1")
                    f_act.wait(pe, cf - 1, f"relu{MT - 1}")
                    for q in range(KM):
                        for b in range(TB):
                            mm = pe.transpose(FB[:, q * CH + b * P:q * CH + (b + 1) * P],
                                              xin[:, b, q * P:(q + 1) * P], ident)
                    f_pe.done(mm, "tr")

                def f_in(r):
                    f_act.wait(pe, cf, "xT" if r == 0 else f"e{r - 1}")
                    for m in range(2):
                        for q in range(KM):
                            c0 = (2 * r + m) * P
                            mm = pe.matmul(FB[:, m * CH:(m + 1) * CH], Win[:, q, c0:c0 + P], xT[:, q, :],
                                           start=(q == 0), stop=(q == KM - 1))
                    f_pe.done(mm, f"ip{r}")

                def f_x():
                    f_act.wait(pe, cf, "silu_x")
                    for m in range(MT):
                        mm = pe.matmul(FB[0:2 * NS + 1, 0:CH], Wx[:, m, :], xc[:, m, :],
                                       start=(m == 0), stop=(m == MT - 1))
                    f_pe.done(mm, "xp")

                def f_dt():
                    f_act.wait(pe, cf, "xd")
                    f_pe.done(pe.matmul(FB[:, CH:2 * CH], SelDt[:, :], xd[:, :], start=True, stop=True), "db")

                def p_out():
                    ld_y2.wait(pe, cp)
                    p_act.wait(pe, cp - 1, "sig")
                    for b in range(TB):
                        for m in range(MT):
                            mm = pe.matmul(PBK[:, b * DM:(b + 1) * DM], y2[:, m, b * P:(b + 1) * P], Wout[:, m, :],
                                           start=(m == 0), stop=(m == MT - 1))
                    p_pe.done(mm, "op")

                def p_turn():
                    p_dve.wait(pe, cp, "x21")
                    for q in range(KM):
                        for b in range(TB):
                            mm = pe.transpose(PBK[:, q * CH + b * P:q * CH + (b + 1) * P],
                                              rn[:, b, q * P:(q + 1) * P], ident)
                    p_pe.done(mm, "tr")

                def p_route():
                    p_act.wait(pe, cp, "x2T")
                    for b in range(TB):
                        for q in range(KM):
                            mm = pe.matmul(PBK[:, b * NE:(b + 1) * NE], x2T[:, q, b * P:(b + 1) * P], Wrt[:, q, :],
                                           start=(q == 0), stop=(q == KM - 1))
                    p_pe.done(mm, "rt")

                at = {}
                if on["F"]:
                    at.update({(3, "F"): [f_turn], (4, "F"): [lambda: f_in(0)], (5, "F"): [lambda: f_in(1)],
                               (6, "F"): [lambda: f_in(2)], (7, "F"): [lambda: f_in(3)],
                               (10, "F"): [f_x], (11, "F"): [f_dt]})
                if on["P"]:
                    at.update({(4, "P"): [p_out], (11, "P"): [p_turn], (12, "P"): [p_route]})
                for n in range(STEPS):
                    if on["M"]:
                        gate_up(n)
                    for f in at.get((n, "F"), []) + at.get((n, "P"), []):
                        f()
                    if on["M"]:
                        if n >= 1:
                            turn(n - 1)
                        if n >= 2:
                            down(n - 2)
                    if on["S"] and n >= 5 and (n - 5) % NBETA == 0:
                        add_states((n - 5) // NBETA)
                if on["M"]:
                    turn(STEPS - 1)
                    down(STEPS - 2)
                    down(STEPS - 1)
                if on["S"]:
                    add_states(NSIG - 1)

            run(pe, body)

        @block.scalar
        def _(act):
            for s in (f_act, s_act, p_act, m_th, m_aT, m_my):
                s.credit(act)
            act.wait_ge(ld_w, 16 * (len(weights) + 1))
            act.activation(ADall[:, :, 0:UNITS], ADall[:, :, 0:UNITS], ACT.Exp).then_inc(w_act, 1)
            act.wait_ge(w_dve, 2)

            def body(k, on, base=0):
                i = k + base
                cf, cp, cm_ = i - FIRST_F, i - FIRST_P, i - FIRST_M

                def decay(n):
                    beta = n % NBETA
                    if n == 0:
                        s_act.wait(act, i - 1, f"dA{UNITS - 1}")
                        s_act.done(act.activation(Acur[:, :], ADall[:, i % MT, 0:UNITS], ACT.Copy), "ad")
                        s_act.wait(act, i, "ad")
                    if n < NBETA:
                        ld_dt[beta].wait(act, i)
                    s_sc.wait(act, i if n >= NA else i - 1, f"h{(n - NA) % UNITS}")
                    s_act.done(act.activation(dA[:, n % NA, :], dtr[:, beta, :], ACT.Exp, scale=Acur[:, n:n + 1]),
                               f"dA{n}")

                def tanh(n):
                    m_pe_g.wait(act, cm_, f"g{n}")
                    m_pe_t.wait(act, cm_ if n >= 2 else cm_ - 1, f"t{(n - 2) % STEPS}")
                    m_th.done(act.activation(th[:, n % 2, :], GU[n % 2][:, 0:2 * DE], ACT.Tanh, scale=0.5), f"th{n}")

                def evac(n):
                    m_pe_t.wait(act, cm_, f"t{n}")
                    m_pe_d.wait(act, cm_ if n >= 2 else cm_ - 1, f"d{(n - 2) % STEPS}")
                    m_aT.done(act.activation(aT[:, n % 2, :], TR[:, 0:2 * DE], ACT.Copy), f"aT{n}")

                def evac_y(b):
                    m_pe_d.wait(act, cm_, f"d{(b + 1) * PAIRS - 1}")
                    z_dve.wait(act, cm_ - 1, "o1")
                    m_my.done(act.activation(my[:, b, :], MY[:, b * DM:(b + 1) * DM], ACT.Copy), f"my{b}")

                def f_xT():
                    f_pe.wait(act, cf, "tr")
                    f_pe.wait(act, cf - 1, "ip3")
                    f_act.done(act.activation(xT[:, :, :], FB[:, :].rearrange("p (q t) -> p q t", q=KM), ACT.Copy), "xT")

                def f_ev(r):
                    f_pe.wait(act, cf, f"ip{r}")
                    src = FB[:, :].rearrange("p (m t) -> p m t", m=2)
                    if r < 2:
                        if r == 0:
                            f_dve.wait(act, cf - 1, "dx")
                            st_dt.wait(act, cf - 1)
                        dst = xb[:, 2 * r:2 * r + 2, HIST:HIST + CH]
                    else:
                        if r == 2:
                            st_xn.wait(act, cf)
                        dst = sz[:, 2 * r - 4:2 * r - 2, :]
                    f_act.done(act.activation(dst, src, ACT.Copy), f"e{r}")

                def f_silu():
                    f_act.wait(act, cf, "e3")
                    f_act.done(act.activation(sz[:, :, :], sz[:, :, :], ACT.Silu), "silu_z")
                    f_dve.wait(act, cf, f"c3{MT - 1}")
                    f_act.done(act.activation(xc[:, :, :], xc[:, :, :], ACT.Silu), "silu_x")

                def f_xd():
                    f_pe.wait(act, cf, "xp")
                    st_xd.wait(act, cf - 1)
                    f_act.done(act.activation(xd[:, :], FB[0:2 * NS + 1, 0:CH], ACT.Copy), "xd")

                def f_sp():
                    f_pe.wait(act, cf, "db")
                    st_sz.wait(act, cf)
                    f_dve.wait(act, cf, "hist")
                    for m in range(MT):
                        wb = dict(scale=dt_w[:, m:m + 1], bias=dt_b[:, m:m + 1])
                        f_act.done(act.activation(sz[:, m, :], FB[:, CH:2 * CH], ACT.Abs, **wb), f"abs{m}")
                        f_act.done(act.activation(dt[:, m, :], FB[:, CH:2 * CH], ACT.Relu, **wb), f"relu{m}")
                    f_act.wait(act, cf, f"abs{MT - 1}")
                    f_act.done(act.activation(sz[:, :, :], sz[:, :, :], ACT.Exp, scale=-1.0), "exp")

                def f_ln():
                    f_dve.wait(act, cf, "lost")
                    f_act.done(act.activation(sz[:, :, :], sz[:, :, :], ACT.Ln, bias=1.0), "ln")

                def p_x2T():
                    p_pe.wait(act, cp, "tr")
                    p_act.wait(act, cp - 1, "cm")
                    p_act.done(act.activation(x2T[:, :, :], PBK[:, :].rearrange("p (q t) -> p q t", q=KM), ACT.Copy), "x2T")

                def p_sig():
                    p_pe.wait(act, cp, "rt")
                    p_dve.wait(act, cp - 1, "comb")
                    p_act.done(act.activation(R[:, 0, :], PBK[:, 0:TB * NE], ACT.Sigmoid), "sig")

                def p_hand():
                    m_pe_g.wait(act, cp - 1, f"g{STEPS - 1}")
                    p_act.wait(act, cp, "x2T")
                    p_act.done(act.activation(x2m[:, :, :], x2T[:, :, :], ACT.Copy), "x2m")
                    m_dve.wait(act, cp - 1, f"f{STEPS - 1}")
                    p_dve.wait(act, cp, "comb")
                    p_act.done(act.activation(cm[:, :], comb[:, :], ACT.Copy), "cm")

                for n in range(STEPS):
                    if on["S"]:
                        decay(n)
                    if on["M"]:
                        tanh(n)
                        if n >= 1:
                            evac(n - 1)
                        if n == PAIRS + 2:
                            evac_y(0)
                    if on["F"]:
                        if n == 3:
                            f_xT()
                        if 4 <= n < 8:
                            f_ev(n - 4)
                        if n == 9:
                            f_silu()
                        if n == 10:
                            f_xd()
                        if n == 12:
                            f_sp()
                        if n == 13:
                            f_ln()
                    if on["P"]:
                        if n == 11:
                            p_x2T()
                        if n == 12:
                            p_sig()
                if on["M"]:
                    evac(STEPS - 1)
                    evac_y(1)
                if on["P"]:
                    p_hand()

            run(act, body)

        @block.gpsimd
        def _(pool):
            s_hc.credit(pool)
            y_pool.credit(pool)
            f_pool.credit(pool)

            def body(k, on, base=0):
                i = k + base
                cf = i - FIRST_F
                for n in range(UNITS):
                    if on["F"] and n == 14:
                        f_act.wait(pool, cf, "ln")
                        f_pool.done(pool.tensor_tensor(low, low, sz[:, :, :], ALU.add), "ln")
                    if on["Y"] and n == 2:
                        y_dve.wait(pool, i - FIRST_Y, "skip1")
                        y_pool.done(pool.tensor_tensor(yt[:, :], yt[:, :], gt[:, :], ALU.mult), "gate")
                    if on["S"]:
                        if n == 0:
                            pass
                        s_sc.wait(pool, i, f"h{n}")
                        if n % NBETA == 0:
                            ld_bc[n // NBETA].wait(pool, i // NCH)
                        h = hs[:, SLOT[n], :]
                        s_hc.done(pool.tensor_tensor(h, h, Cb[:, n // NBETA, :], ALU.mult), f"c{n}")

            run(pool, body)

        @block.vector
        def _(dve):
            for s in (f_dve, s_u, s_sc, y_dve, p_dve, m_dve, z_dve):
                s.credit(dve)
            dve.wait_ge(ld_w, 16 * (len(weights) + 1))
            for q in range(KM):
                ins = dve.tensor_scalar(Win[:, q, :], Win[:, q, :], norm_w[:, q:q + 1], None, ALU.mult)
            ins.then_inc(w_dve, 1)
            dve.wait_ge(w_act, 1)
            dve.tensor_scalar(ADall[:, :, 0:UNITS], ADall[:, :, 0:UNITS], -1.0, None, ALU.mult).then_inc(w_dve, 1)
            dve.memset(xb[:, :, :], 0.0).then_inc(w_dve, 1)
            dve.wait_ge(w_dve, 3)

            def body(k, on, base=0):
                i = k + base
                cf, cp, cm_, cz, iy = i - FIRST_F, i - FIRST_P, i - FIRST_M, i - FIRST_Z, i - FIRST_Y

                def op(steps, it, name, emit, *after):
                    for a in after[-1:]:
                        steps.wait(dve, it, a)
                    steps.done(emit(), name)

                def rsqrt(steps, it, tag, w, after):
                    v, y, a = w[:, 0, :], w[:, 1, :], w[:, 2, :]
                    op(steps, it, f"{tag}_half", lambda: dve.tensor_scalar(
                        a.bitcast(I32), v.bitcast(I32), 1, None, ALU.logical_shift_right), after)
                    yield
                    op(steps, it, f"{tag}_guess", lambda: dve.tensor_scalar(
                        y.bitcast(I32), a.bitcast(I32), -1.0, RSQRT_MAGIC, ALU.mult, ALU.add), f"{tag}_half")
                    yield
                    last = f"{tag}_guess"
                    for n in range(3):
                        op(steps, it, f"{tag}_a{n}", lambda: dve.scalar_tensor_tensor(
                            out=a, in0=y, scalar=-0.5, in1=y, op0=ALU.mult, op1=ALU.mult), last)
                        yield
                        op(steps, it, f"{tag}_b{n}", lambda: dve.tensor_tensor(a, a, v, ALU.mult), f"{tag}_a{n}")
                        yield
                        op(steps, it, f"{tag}_y{n}", lambda: dve.scalar_tensor_tensor(
                            out=y, in0=a, scalar=1.5, in1=y, op0=ALU.add, op1=ALU.mult), f"{tag}_b{n}")
                        last = f"{tag}_y{n}"
                        yield

                def stats(steps, it, pre, src, st, mv, after):
                    for b in range(TB):
                        op(steps, it, f"{pre}bn{b}", lambda: dve.bn_stats(st[:, b, :], src[:, b, :]), *after)
                        yield
                    op(steps, it, f"{pre}both", lambda: dve.memset(mark[:, :], 0.0), f"{pre}bn1")
                    for b in range(TB):
                        op(steps, it, f"{pre}ag{b}", lambda: dve.bn_aggr(mv[:, b, :], st[:, b, :]))
                        yield

                def part_f():
                    ld_xin.wait(dve, cf)
                    yield from stats(f_dve, cf, "", xin, f_st, f_mv, ())
                    op(f_dve, cf, "w1", lambda: dve.tensor_scalar(f_w[:, 0, 0:TB], f_mv[:, :, 1], LN_EPS, None, ALU.add), "ag1")
                    yield
                    op(f_dve, cf, "w2", lambda: dve.tensor_scalar(
                        f_w[:, 0, TB:2 * TB], f_mv[:, :, 1], 1.0 + RMS_EPS, LN_EPS * RMS_EPS, ALU.mult, ALU.add))
                    yield
                    yield from rsqrt(f_dve, cf, "r", f_w, "w2")
                    f_pool.wait(dve, cf - 1, "ln")
                    for b in range(TB):
                        op(f_dve, cf, f"xn{b}", lambda: dve.tensor_scalar(
                            xn[:, b, :], xin[:, b, :], f_mv[:, b, 0:1], f_w[:, 1, b:b + 1], ALU.subtract, ALU.mult), "r_y2")
                        yield
                    for b in range(TB):
                        op(f_dve, cf, f"xr{b}", lambda: dve.tensor_scalar(
                            xin[:, b, :], xin[:, b, :], f_mv[:, b, 0:1], f_w[:, 1, TB + b:TB + b + 1],
                            ALU.subtract, ALU.mult))
                        yield

                def part_f2():
                    st_dx.wait(dve, cf - 1)
                    f_act.wait(dve, cf, "e1")
                    for t in range(TAPS):
                        for m in range(MT):
                            src = xb[:, m, t:t + CH]
                            if t == 0:
                                op(f_dve, cf, f"c{t}{m}", lambda: dve.tensor_scalar(
                                    xc[:, m, :], src, conv_w[:, m, t:t + 1], conv_b[:, m:m + 1], ALU.mult, ALU.add))
                            else:
                                op(f_dve, cf, f"c{t}{m}", lambda: dve.scalar_tensor_tensor(
                                    out=xc[:, m, :], in0=src, scalar=conv_w[:, m, t:t + 1], in1=xc[:, m, :],
                                    op0=ALU.mult, op1=ALU.add), f"c{t - 1}{m}")
                            yield
                    op(f_dve, cf, "hist", lambda: dve.tensor_scalar(
                        xb[:, :, 0:HIST], xb[:, :, CH:CH + HIST], kp[:, 0:1], None, ALU.mult))
                    yield

                def part_f3():
                    f_act.wait(dve, cf, "exp")
                    op(f_dve, cf, "near", lambda: dve.tensor_scalar(low, sz[:, :, :], 1.0, -1.0, ALU.add, ALU.add))
                    yield
                    op(f_dve, cf, "lost", lambda: dve.tensor_tensor(low, sz[:, :, :], low, ALU.subtract), "near")
                    yield
                    f_pool.wait(dve, cf, "ln")
                    op(f_dve, cf, "dt", lambda: dve.tensor_tensor(dt, dt, low, ALU.add))
                    yield
                    st_xc.wait(dve, cf)
                    f_pe.wait(dve, cf, "xp")
                    op(f_dve, cf, "dx", lambda: dve.tensor_tensor(xc[:, :, :], dt, xc[:, :, :], ALU.mult), "dt")
                    yield

                def inputs(n):
                    s, beta = divmod(n, NBETA)
                    if s == 0:
                        ld_dt[beta].wait(dve, i)
                    if beta == 0:
                        ld_bc[s].wait(dve, i // NCH)
                    back, m = slot_before(n)
                    s_pe.wait(dve, i + back, f"y{m // NBETA}")
                    s_u.done(dve.tensor_tensor(hs[:, SLOT[n], :], dxr[:, beta, :], Bb[:, s, :], ALU.mult), f"u{n}")

                def scan(n):
                    s_act.wait(dve, i, f"dA{n}")
                    s_u.wait(dve, i, f"u{n}")
                    s_sc.done(dve.tensor_tensor_scan(hs[:, SLOT[n], :], dA[:, n % NA, :], hs[:, SLOT[n], :], 0.0,
                                                     ALU.mult, ALU.add), f"h{n}")

                def part_y():
                    s_pe.wait(dve, iy, f"y{NSIG - 1}")
                    ld_yt.wait(dve, iy)
                    for h in range(2):
                        op(y_dve, iy, f"skip{h}", lambda: dve.scalar_tensor_tensor(
                            out=yt[:, h * 512:(h + 1) * 512], in0=yt[:, h * 512:(h + 1) * 512],
                            scalar=ADall[:, iy % MT, UNITS:UNITS + 1], in1=Y[h][:, :], op0=ALU.mult, op1=ALU.add))
                        yield

                def part_p():
                    p_pe.wait(dve, cp, "op")
                    ld_p.wait(dve, cp)
                    op(p_dve, cp, "r", lambda: dve.tensor_tensor(
                        rn[:, :, :], PBK[:, :].rearrange("p (b h) -> p b h", b=TB), rn[:, :, :], ALU.add))
                    yield
                    yield from stats(p_dve, cp, "", rn, p_st, p_mv, ("r",))
                    op(p_dve, cp, "w1", lambda: dve.tensor_scalar(p_w[:, 0, :], p_mv[:, :, 1], LN_EPS, None, ALU.add), "ag1")
                    yield
                    yield from rsqrt(p_dve, cp, "r", p_w, "w1")
                    for b in range(TB):
                        op(p_dve, cp, f"o{b}", lambda: dve.tensor_scalar(
                            rn[:, b, :], rn[:, b, :], p_mv[:, b, 0:1], p_w[:, 1, b:b + 1], ALU.subtract, ALU.mult), "r_y2")
                        yield
                    op(p_dve, cp, "x1", lambda: dve.tensor_tensor(x1[:, :, :], rn[:, :, :], x1[:, :, :], ALU.add), "o1")
                    yield
                    yield from stats(p_dve, cp, "B", x1, p_st, p_mv, ("x1",))
                    op(p_dve, cp, "Bw1", lambda: dve.tensor_scalar(p_w[:, 0, :], p_mv[:, :, 1], LN_EPS, None, ALU.add), "Bag1")
                    yield
                    yield from rsqrt(p_dve, cp, "q", p_w, "Bw1")
                    for b in range(TB):
                        op(p_dve, cp, f"x2{b}", lambda: dve.tensor_scalar(
                            rn[:, b, :], x1[:, b, :], p_mv[:, b, 0:1], p_w[:, 1, b:b + 1], ALU.subtract, ALU.mult), "q_y2")
                        yield

                def part_p2():
                    p_act.wait(dve, cp, "sig")
                    G = TB * NG
                    score, sfc, tmp, w = (R[:, k, :] for k in (0, 1, 2, 3))
                    q4 = sfc.rearrange("p (g e) -> p g e", e=NE // NG)
                    hi, lo = (R[:, k, 0:2 * G].rearrange("p (g e) -> p g e", e=2) for k in (4, 5))
                    top1, ta, tb, gs, gr = (R[:, 6, k * G:(k + 1) * G] for k in (0, 1, 2, 3, 1))
                    gm = R[:, 7, 0:G]
                    rk = R[:, 8, :]
                    ws, wr = R[:, 9, 0:TB], R[:, 9, TB:2 * TB]
                    gg, ge = (R[:, k, :].rearrange("p (b i j) -> p b i j", b=TB, i=NG) for k in (10, 11))
                    tt = dve.tensor_tensor
                    o = lambda name, emit, *after: op(p_dve, cp, name, emit, *after)
                    o("sfc", lambda: tt(sfc, score, Ebias[:, :], ALU.add)); yield
                    o("hi", lambda: tt(hi, q4[:, :, 0:2], q4[:, :, 2:4], ALU.max), "sfc"); yield
                    o("lo", lambda: tt(lo, q4[:, :, 0:2], q4[:, :, 2:4], ALU.min)); yield
                    o("t1", lambda: tt(top1, hi[:, :, 0], hi[:, :, 1], ALU.max), "lo"); yield
                    o("t2a", lambda: tt(ta, hi[:, :, 0], hi[:, :, 1], ALU.min)); yield
                    o("t2b", lambda: tt(tb, lo[:, :, 0], lo[:, :, 1], ALU.max)); yield
                    o("t2", lambda: tt(tb, ta, tb, ALU.max), "t2b"); yield
                    o("gs", lambda: tt(gs, top1, tb, ALU.add), "t2"); yield
                    gv = gs.rearrange("p (b g) -> p b g", b=TB)
                    g_j = gv.unsqueeze(2).broadcast_to([P, TB, NG, NG])
                    g_i = gv.unsqueeze(3).broadcast_to([P, TB, NG, NG])
                    bg = before_g.rearrange("p (i j) -> p i j", i=NG).unsqueeze(1).broadcast_to([P, TB, NG, NG])
                    o("ggt", lambda: tt(gg, g_j, g_i, ALU.is_gt), "gs"); yield
                    o("geq", lambda: tt(ge, g_j, g_i, ALU.is_equal)); yield
                    o("gq", lambda: tt(ge, ge, bg, ALU.mult), "geq"); yield
                    o("ga", lambda: tt(gg, gg, ge, ALU.add), "gq"); yield
                    o("gr", lambda: dve.tensor_reduce(gr, R[:, 10, :].rearrange("p (g j) -> p g j", j=NG), AX.X, ALU.add), "ga"); yield
                    o("gm", lambda: dve.tensor_scalar(gm, gr, float(TOPG), None, ALU.is_lt), "gr"); yield
                    t4 = tmp.rearrange("p (g e) -> p g e", e=NE // NG)
                    o("tmp", lambda: tt(t4, q4, gm.unsqueeze(2).broadcast_to([P, G, NE // NG]), ALU.mult), "gm"); yield
                    tv = tmp.rearrange("p (b e) -> p b e", b=TB)
                    e_j = tv.unsqueeze(2).broadcast_to([P, TB, NE, NE])
                    e_i = tv.unsqueeze(3).broadcast_to([P, TB, NE, NE])
                    gt_, eq_ = (RR[:, k, :].rearrange("p (b i j) -> p b i j", b=TB, i=NE) for k in (0, 1))
                    be = before.rearrange("p (i j) -> p i j", i=NE).unsqueeze(1).broadcast_to([P, TB, NE, NE])
                    o("gt", lambda: tt(gt_, e_j, e_i, ALU.is_gt), "tmp"); yield
                    o("eq", lambda: tt(eq_, e_j, e_i, ALU.is_equal)); yield
                    o("eqb", lambda: tt(eq_, eq_, be, ALU.mult), "eq"); yield
                    o("ad", lambda: tt(RR[:, 0, :], RR[:, 0, :], RR[:, 1, :], ALU.add), "eqb"); yield
                    o("rk", lambda: dve.tensor_reduce(rk, RR[:, 0, :].rearrange("p (r j) -> p r j", j=NE), AX.X, ALU.add), "ad"); yield
                    o("w", lambda: dve.scalar_tensor_tensor(out=w, in0=rk, scalar=float(TOPK), in1=score,
                                                            op0=ALU.is_lt, op1=ALU.mult), "rk"); yield
                    wv = w.rearrange("p (b e) -> p b e", b=TB)
                    o("ws", lambda: dve.tensor_reduce(ws, wv, AX.X, ALU.add), "w"); yield
                    o("we", lambda: dve.tensor_scalar(ws, ws, 1e-20, None, ALU.add), "ws"); yield
                    o("wr", lambda: dve.reciprocal(wr, ws), "we"); yield
                    p_act.wait(dve, cp - 1, "cm")
                    op(p_dve, cp, "comb", lambda: dve.scalar_tensor_tensor(
                        out=comb[:, :].rearrange("p (b e) -> p b e", b=TB), in0=wv, scalar=0.5,
                        in1=wr.unsqueeze(2).broadcast_to([P, TB, NE]), op0=ALU.mult, op1=ALU.mult), "wr")
                    yield

                def expert(n):
                    b, p = divmod(n, PAIRS)
                    g = GU[n % 2]
                    m_th.wait(dve, cm_, f"th{n}")
                    op(m_dve, cm_, f"a{n}", lambda: dve.scalar_tensor_tensor(
                        out=th[:, n % 2, :], in0=th[:, n % 2, :], scalar=1.0, in1=g[:, 0:2 * DE],
                        op0=ALU.add, op1=ALU.mult))
                    if n == 0:
                        p_act.wait(dve, cm_, "cm")
                    for e, name in enumerate("ef"):
                        c = b * NE + 2 * p + e
                        sl = slice(e * DE, (e + 1) * DE)
                        op(m_dve, cm_, f"{name}{n}", lambda: dve.scalar_tensor_tensor(
                            out=th[:, n % 2, sl], in0=g[:, (2 + e) * DE:(3 + e) * DE], scalar=cm[:, c:c + 1],
                            in1=th[:, n % 2, sl], op0=ALU.mult, op1=ALU.mult), f"a{n}")

                def part_z():
                    m_my.wait(dve, cz, f"my{TB - 1}")
                    ld_x1.wait(dve, cz)
                    yield from stats(z_dve, cz, "", my, z_st, z_mv, ())
                    op(z_dve, cz, "w1", lambda: dve.tensor_scalar(z_w[:, 0, :], z_mv[:, :, 1], LN_EPS, None, ALU.add), "ag1")
                    yield
                    yield from rsqrt(z_dve, cz, "r", z_w, "w1")
                    for b in range(TB):
                        op(z_dve, cz, f"o{b}", lambda: dve.tensor_scalar(
                            my[:, b, :], my[:, b, :], z_mv[:, b, 0:1], z_w[:, 1, b:b + 1], ALU.subtract, ALU.mult), "r_y2")
                        yield
                    op(z_dve, cz, "out", lambda: dve.tensor_tensor(x1m[:, :, :], my[:, :, :], x1m[:, :, :], ALU.add), "o1")
                    yield

                def pull(gen, n):
                    for _ in range(n):
                        if next(gen, "end") == "end":
                            return

                f1, f2, f3 = part_f(), part_f2(), part_f3()
                p1, p2, z = part_p(), part_p2(), part_z()
                for n in range(UNITS):
                    if on["S"]:
                        inputs(n)
                    if on["Y"] and n == 1:
                        pull(part_y(), 9)
                    if on["S"]:
                        scan(n)
                    if on["M"]:
                        expert(n)
                    if on["F"]:
                        if n <= 3:
                            pull(f1, 7 if n < 3 else 99)
                        if 7 <= n <= 9:
                            pull(f2, 6 if n < 9 else 99)
                        if n in (12, 13, 15):
                            pull(f3, 1 if n < 15 else 9)
                    if on["P"]:
                        if 5 <= n <= 11:
                            pull(p1, 6 if n < 11 else 99)
                        if n >= 13:
                            pull(p2, 9 if n < 15 else 99)
                    if on["Z"] and 1 <= n <= 4:
                        pull(z, 6 if n < 4 else 99)

            run(dve, body)


def kernel(**inputs):
    import concourse.bacc as bacc
    from concourse.bass_utils import run_bass_kernel_spmd

    g = {k.removeprefix("L0_"): np.asarray(v) for k, v in inputs.items()}
    tiles = lambda a: np.ascontiguousarray(a.reshape(-1, P, *a.shape[1:]).swapaxes(0, 1))
    eye = np.eye(P, dtype=np.float32)
    order = list(range(1, 2 * NS + 1)) + [0]
    gate = g["ffn_gate_proj"].transpose(2, 0, 1).reshape(DM, PAIRS, 2 * DE)
    up = g["ffn_up_proj"].transpose(2, 0, 1).reshape(DM, PAIRS, 2 * DE)
    alog = g["attn_A_log"].reshape(MT, NBETA, CB, NSIG, SG).transpose(4, 2, 0, 3, 1).reshape(P, MT, UNITS)
    col = lambda a: tiles(a.reshape(DI, 1))[:, :, 0]
    conv = tiles(g["attn_conv_w"].reshape(DI, TAPS)).reshape(P, MT * TAPS)
    i_, j_ = np.arange(NE), np.arange(NG)
    before = (i_[None, :] < i_[:, None]).astype(np.float32).reshape(1, -1)
    before_g = (j_[None, :] < j_[:, None]).astype(np.float32).reshape(1, -1)
    sel_dt = np.zeros((2 * NS + 1, P), np.float32)
    sel_dt[2 * NS] = 1.0
    keep = np.ones((NCH, P, 1), np.float32)
    keep[NCH - 1] = 0.0
    arrays = dict(
        x=np.ascontiguousarray(g["attn_x"].reshape(BATCH * SEQ, DM)),
        w_in=tiles(g["attn_in_proj_w"]),
        w_out=tiles(g["attn_out_proj_w"]),
        w_gu=tiles(np.concatenate([gate, up], axis=2)),
        w_dn=np.ascontiguousarray(g["ffn_down_proj"].transpose(2, 0, 1)),
        w_x=tiles(g["attn_x_proj_w"][:, order]),
        w_rt=tiles(np.ascontiguousarray(g["ffn_gate_weight"].T)),
        cols=np.concatenate([conv, col(g["attn_conv_b"]), col(g["attn_dt_proj_w"]), col(g["attn_dt_proj_b"]),
                             col(g["attn_D"]), tiles(g["attn_norm_w"].reshape(DM, 1))[:, :, 0]], axis=1),
        alog=np.concatenate([alog, col(g["attn_D"])[:, :, None]], axis=2),
        ebias=np.broadcast_to(np.tile(g["ffn_e_bias"], TB), (P, TB * NE)),
        consts=np.concatenate([eye, np.tile(np.eye(CB, dtype=np.float32), (SG, 1)),
                               np.broadcast_to(before, (P, NE * NE)), np.broadcast_to(before_g, (P, NG * NG))], axis=1),
        sel_dt=sel_dt,
        keep=keep,
    )
    nc = bacc.Bacc("TRN2", target_bir_lowering=False, num_devices=1)
    feed, args = {}, []
    for name, a in arrays.items():
        a = np.ascontiguousarray(a)
        feed[f"in_{name}"] = a
        args.append(nc.dram_tensor(f"in_{name}", a.shape, mybir.dt.from_np(a.dtype), kind="ExternalInput").ap())
    o = nc.dram_tensor("out_0", (BATCH * SEQ, DM), F32, kind="ExternalOutput").ap()
    sandwich_kernel(nc, *args, o)
    r = run_bass_kernel_spmd(nc, [feed], core_ids=[0])
    return r.results[0]["out_0"].reshape(BATCH, SEQ, DM)
```

```python
from contextlib import ExitStack

import numpy as np
import concourse.bass as bass
from concourse import mybir

F32 = mybir.dt.float32
I32 = mybir.dt.int32
ALU = mybir.AluOpType
ACT = mybir.ActivationFunctionType
AX = mybir.AxisListType

P = 128
BATCH, SEQ, DM = 8, 1024, 256
DI, NS, TAPS = 512, 16, 4
NE, NG, DE, TOPK, TOPG = 16, 4, 128, 4, 2
CH = 256
TB = CH // P
KM = DM // P
MT = DI // P
NCH = SEQ // CH
NTILE = BATCH * MT
SG = 4
CB = P // SG
NSIG = NS // SG
NBETA = P // CB
UNITS = NSIG * NBETA
NA, NH, NTH = 2, 6, 3
SLOT = [0, 1, 2, 3, 4, 5, 0, 1, 2, 3, 0, 1, 4, 5, 2, 3]
POOL_BETAS = (1, 3)
PAIRS = NE // 2
STEPS = TB * PAIRS
TH = [n % NTH for n in range(STEPS - 1)] + [1]
HIST = TAPS - 1
assert len(SLOT) == UNITS == STEPS == len(TH)
LN_EPS, RMS_EPS = 1e-5, 1e-6
RSQRT_MAGIC = float(0x5F3759DF)

FIRST_F, FIRST_S, FIRST_Y, FIRST_P, FIRST_M, FIRST_Z = -NCH, 0, 1, NCH, NCH + 1, NCH + 2
PARTS = dict(F=FIRST_F, S=FIRST_S, Y=FIRST_Y, P=FIRST_P, M=FIRST_M, Z=FIRST_Z)


ALL = 99
PLAN = {1: dict(Y=2, F1=11), 2: dict(F1=ALL), 3: dict(Z=7), 4: dict(Z=7), 5: dict(Z=ALL, P1=2),
        6: dict(P1=7, F2=4), 7: dict(P1=7, F2=6), 8: dict(P1=8, F2=ALL), 9: dict(P1=8), 10: dict(P1=ALL),
        12: dict(F3=2), 13: dict(P2=9), 14: dict(P2=9), 15: dict(F3=ALL, P2=ALL)}


def segments():
    cuts = sorted({f for f in PARTS.values()} | {f + NTILE for f in PARTS.values()})
    out = []
    for a, b in zip(cuts, cuts[1:]):
        out.append((a, b, {p: f <= a < f + NTILE for p, f in PARTS.items()}))
    return out


def rsqrt_names(tag):
    return [f"{tag}_half", f"{tag}_guess"] + [f"{tag}_{s}{n}" for n in range(3) for s in ("a", "b", "y")]


TICK = {}


def settle(eng):
    if eng is TICK.get("engine"):
        eng.sem_inc(TICK["sem"], 1)


class Steps:

    def __init__(self, sem, names):
        self.sem, self.names, self.per, self.at = sem, names, len(names), 0
        assert len(set(names)) == len(names)

    def credit(self, eng):
        eng.sem_inc(self.sem, self.per)

    def done(self, ins, name):
        assert self.names[self.at % self.per] == name, (name, self.names[self.at % self.per])
        self.at += 1
        ins.then_inc(self.sem, 1)

    def wait(self, eng, it, name):
        eng.wait_ge(self.sem, it * self.per + (self.per + self.names.index(name) + 1))
        settle(eng)


def user_before(slots, n):
    m = n - 1
    while slots[m % len(slots)] != slots[n]:
        m -= 1
    return divmod(m, len(slots))


class Moves:

    def __init__(self, sem, n=1):
        self.sem, self.per = sem, 16 * n

    def credit(self, eng):
        eng.sem_inc(self.sem, self.per)

    def add(self, ins):
        ins.then_inc(self.sem, 16)

    def wait(self, eng, it):
        eng.wait_ge(self.sem, it * self.per + 2 * self.per)
        settle(eng)


def sandwich_kernel(nc, x, w_in, w_out, w_gu, w_dn, w_x, w_rt, cols, alog, ebias, consts, sel_dt, keep, out):
    with ExitStack() as ctx:
        def sb(name, shape, dt=F32):
            return ctx.enter_context(nc.sbuf_tensor(name, shape, dt))

        def pb(name):
            return ctx.enter_context(nc.psum_tensor(name, [P, 512], F32))

        def sem(name):
            return ctx.enter_context(nc.semaphore(name))

        def scratch(name, shape):
            return nc.dram_tensor(name, shape, F32, kind="Internal").ap()

        dt_d = scratch("dt_d", (BATCH * DI, SEQ))
        dx_d = scratch("dx_d", (BATCH * DI, SEQ))
        xc_d = scratch("xc_d", (BATCH * DI, SEQ))
        sz_d = scratch("sz_d", (BATCH * DI, SEQ))
        y_d = scratch("y_d", (BATCH * DI, SEQ))
        bc_d = scratch("bc_d", (BATCH * 2 * NS, SEQ))
        xn_d = scratch("xn_d", (BATCH * SEQ, DM))
        x1_d = scratch("x1_d", (BATCH * SEQ, DM))

        def tokens(t, c):
            return t.rearrange("(c b p) h -> c p b h", b=TB, p=P)[c]

        def chunk(t, b, j):
            return t.rearrange("(b m p) (j t) -> b j p m t", m=MT, p=P, j=NCH)[b, j]

        def tile_of(t, i):
            return t.rearrange("(i p) t -> i p t", p=P)[i]

        Win = sb("Win", [P, KM, 2 * DI])
        Wout = sb("Wout", [P, MT, DM])
        Wgu = sb("Wgu", [P, KM, PAIRS, 4 * DE])
        Wdn = sb("Wdn", [P, NE, DM])
        Wx = sb("Wx", [P, MT, 2 * NS + 1])
        Wrt = sb("Wrt", [P, KM, NE])
        Cols = sb("Cols", [P, MT * (TAPS + 4) + KM])
        ADall = sb("ADall", [P, MT, UNITS + 1])
        Acur = sb("Acur", [P, UNITS])
        Ebias = sb("Ebias", [P, TB * NE])
        Cst = sb("Cst", [P, P + CB + NE * NE + NG * NG])
        SelDt = sb("SelDt", [2 * NS + 1, P])
        conv_w = Cols[:, 0:MT * TAPS].rearrange("p (m k) -> p m k", m=MT)
        conv_b, dt_w, dt_b, d_col = (Cols[:, MT * (TAPS + k):MT * (TAPS + k + 1)] for k in range(4))
        norm_w = Cols[:, MT * (TAPS + 4):MT * (TAPS + 4) + KM]
        ident = Cst[:, 0:P]
        sel_y = Cst[:, P:P + CB]
        before = Cst[:, P + CB:P + CB + NE * NE]
        before_g = Cst[:, P + CB + NE * NE:P + CB + NE * NE + NG * NG]

        fa = sb("fa", [P, 2 * TB * DM])
        xin = fa[:, 0:TB * DM].rearrange("p (b h) -> p b h", b=TB)
        xT = fa[:, TB * DM:].rearrange("p (q t) -> p q t", q=KM)
        low = fa[:, :].rearrange("p (m t) -> p m t", m=MT)
        xb = sb("xb", [P, MT, HIST + CH])
        xc = sb("xc", [P, MT, CH])
        sz = sb("sz", [P, MT, CH])
        xn = sz[:, 0:2, :]
        assert DM == CH and TB == 2
        dt = xb[:, :, HIST:HIST + CH]
        xd = sb("xd", [2 * NS + 1, CH])
        kp = sb("kp", [P, 1])
        f_st = sb("f_st", [P, TB, 6])
        f_mv = sb("f_mv", [P, TB, 2])
        f_w = sb("f_w", [P, 3, 2 * TB])
        mark = sb("mark", [P, 1])
        dtr = sb("dtr", [P, NBETA, SEQ])
        dxr = sb("dxr", [P, NBETA, SEQ])
        Bb = sb("Bb", [P, NSIG, SEQ])
        Cb = sb("Cb", [P, NSIG, SEQ])
        dA = sb("dA", [P, NA, SEQ])
        hs = sb("hs", [P, NH, SEQ])
        yt = sb("yt", [P, SEQ])
        gt = sb("gt", [P, SEQ])
        y2 = sb("y2", [P, MT, CH])
        rn = sb("rn", [P, TB, DM])
        x1 = sb("x1", [P, TB, DM])
        x2T = sb("x2T", [P, KM, CH])
        p_st = sb("p_st", [P, TB, 6])
        p_mv = sb("p_mv", [P, TB, 2])
        p_w = sb("p_w", [P, 3, TB])
        R = rn[:, :, :].rearrange("p b h -> p (b h)")[:, 0:12 * TB * NE].rearrange("p (k e) -> p k e", k=12)
        assert MT * CH == 2 * TB * NE * NE
        RR = y2[:, :, :].rearrange("p (k m) t -> p k (m t)", k=2)
        comb = sb("comb", [P, TB * NE])
        x2m = sb("x2m", [P, KM, CH])
        cm = sb("cm", [P, TB * NE])
        th = sb("th", [P, NTH, 2 * DE])
        aT = sb("aT", [P, 2, 2 * DE])
        my = sb("my", [P, TB, DM])
        x1m = sb("x1m", [P, TB, DM])
        z_st = sb("z_st", [P, TB, 6])
        z_mv = sb("z_mv", [P, TB, 2])
        z_w = sb("z_w", [P, 3, TB])

        Y = [pb("Y0"), pb("Y1")]
        GU = [pb("GU0"), pb("GU1")]
        TR, MY, FB, PBK = pb("TR"), pb("MY"), pb("FB"), pb("PBK")

        f_dve = Steps(sem("f_dve"), ["bn0", "bn1", "both", "ag0", "ag1", "w1", "w2"] + rsqrt_names("r")
                      + ["xn0", "xn1", "xr0", "xr1"] + [f"c{k}{m}" for k in range(TAPS) for m in range(MT)]
                      + ["hist", "near", "lost", "dt", "dx"])
        f_pool = Steps(sem("f_pool"), ["ln"])
        f_pe = Steps(sem("f_pe"), ["tr", "ip0", "ip1", "ip2", "ip3", "xp", "db"])
        f_act = Steps(sem("f_act"), ["xT", "e0", "e1", "e2", "e3", "silu_z", "silu_x", "xd"]
                      + [f"{k}{m}" for m in range(MT) for k in ("abs", "relu")] + ["exp", "ln"])
        s_act = Steps(sem("s_act"), ["ad"] + [f"dA{n}" for n in range(UNITS)])
        s_u = Steps(sem("s_u"), [f"u{n}" for n in range(UNITS) if n % NBETA not in POOL_BETAS])
        s_up = Steps(sem("s_up"), [f"u{n}" for n in range(UNITS) if n % NBETA in POOL_BETAS])
        s_sc = Steps(sem("s_sc"), [f"h{n}" for n in range(UNITS)])
        s_hc = Steps(sem("s_hc"), [f"c{n}" for n in range(UNITS)])
        s_pe = Steps(sem("s_pe"), [f"y{s}" for s in range(NSIG)])
        y_dve = Steps(sem("y_dve"), ["skip0", "skip1"])
        y_pool = Steps(sem("y_pool"), ["gate"])
        route = (["sfc", "hi", "lo", "t1", "t2a", "t2b", "t2", "gs", "ggt", "geq", "gq", "ga", "gr", "gm",
                  "tmp", "gt", "eq", "eqb", "ad", "rk", "w", "ws", "we", "wr", "comb"])
        p_dve = Steps(sem("p_dve"), ["r", "bn0", "bn1", "both", "ag0", "ag1", "w1"] + rsqrt_names("r") + ["o0", "o1", "x1"]
                      + ["Bbn0", "Bbn1", "Bboth", "Bag0", "Bag1", "Bw1"] + rsqrt_names("q") + ["x20", "x21"] + route)
        p_pe = Steps(sem("p_pe"), ["op", "tr", "rt"])
        p_act = Steps(sem("p_act"), ["x2T", "sig"])
        m_in = Steps(sem("m_in"), ["x2m", "cm"])
        m_pe_g = Steps(sem("m_pe_g"), [f"g{n}" for n in range(STEPS)])
        m_pe_t = Steps(sem("m_pe_t"), [f"t{n}" for n in range(STEPS)])
        m_pe_d = Steps(sem("m_pe_d"), [f"d{n}" for n in range(STEPS)])
        m_th = Steps(sem("m_th"), [f"th{n}" for n in range(STEPS)])
        m_aT = Steps(sem("m_aT"), [f"aT{n}" for n in range(STEPS)])
        m_my = Steps(sem("m_my"), [f"my{b}" for b in range(TB)])
        m_dve = Steps(sem("m_dve"), [s for n in range(STEPS) for s in (f"a{n}", f"e{n}", f"f{n}")])
        z_dve = Steps(sem("z_dve"), ["bn0", "bn1", "both", "ag0", "ag1", "w1"] + rsqrt_names("r") + ["o0", "o1", "out"])

        ld_w = sem("ld_w")
        w_act, w_dve = sem("w_act"), sem("w_dve")
        ld_xin = Moves(sem("ld_xin"), 2)
        ld_dt = [Moves(sem(f"ld_dt{b}"), 2) for b in range(NBETA)]
        ld_bc = [Moves(sem(f"ld_bc{s}"), 2) for s in range(NSIG)]
        ld_yt, ld_y2, ld_p, ld_x1 = Moves(sem("ld_yt"), 2), Moves(sem("ld_y2")), Moves(sem("ld_p"), 2), Moves(sem("ld_x1"))
        st_xn, st_sz, st_xc, st_xd, st_dt, st_dx = (Moves(sem(f"st_{k}")) for k in ("xn", "sz", "xc", "xd", "dt", "dx"))
        st_y, st_x1, st_out = (Moves(sem(f"st_{k}")) for k in ("y", "x1", "out"))

        def of_u(beta):
            return s_up if beta in POOL_BETAS else s_u

        block = ctx.enter_context(nc.Block())

        weights = [(Win, w_in), (Cols, cols), (Cst, consts), (Wx, w_x), (SelDt, sel_dt), (Wout, w_out), (Wrt, w_rt),
                   (Ebias, ebias), (Wgu, w_gu), (Wdn, w_dn)]

        @block.sync
        def _(sp):
            TICK.update(engine=sp, sem=sem("sp_tick"))
            for m in (ld_xin, *ld_dt, *ld_bc, ld_yt, ld_y2, ld_p, ld_x1,
                      st_xn, st_sz, st_xc, st_xd, st_dt, st_dx, st_y, st_x1, st_out):
                m.credit(sp)
            sp.dma_start(ADall[:, :, :], alog).then_inc(ld_w, 16)
            for t, src in weights:
                full = t[tuple(slice(None) for _ in src.shape)]
                sp.dma_start(full, src).then_inc(ld_w, 16)

            def load_tile(i, betas=range(NBETA)):
                for beta in betas:
                    rows = slice(beta * CB, (beta + 1) * CB)
                    s_act.wait(sp, i - 1, f"dA{UNITS - NBETA + beta}")
                    ld_dt[beta].add(sp.dma_start(dtr[:, beta, :], tile_of(dt_d, i)[rows, :].partition_broadcast(SG)))
                    of_u(beta).wait(sp, i - 1, f"u{UNITS - NBETA + beta}")
                    ld_dt[beta].add(sp.dma_start(dxr[:, beta, :], tile_of(dx_d, i)[rows, :].partition_broadcast(SG)))

            def load_bc(b, sigmas=range(NSIG)):
                last = b * NCH - 1
                for s in sigmas:
                    end = (s + 1) * NBETA - 1
                    for k, t in enumerate((Bb, Cb)):
                        if k == 0:
                            for steps in (s_u, s_up):
                                steps.wait(sp, last, [u for u in steps.names if int(u[1:]) <= end][-1])
                        else:
                            s_hc.wait(sp, last, f"c{end}")
                        src = bc_d.rearrange("(b k s g) t -> b k s g t", b=BATCH, k=2, g=SG)[b, k, s]
                        ld_bc[s].add(sp.dma_start(t[:, s, :], src.unsqueeze(1).broadcast_to([SG, CB, SEQ])))

            def body(b, j, on, fetch, ends_row):
                i = b * NCH + j
                cf, cp, cz = i - FIRST_F, i - FIRST_P, i - FIRST_Z
                if on["F"]:
                    f_dve.wait(sp, cf - 1, "dt")
                    ld_xin.add(sp.dma_start(xin[:, :, :], tokens(x, cf)))
                    ld_xin.add(sp.dma_start(kp[:, :], keep[j]))
                if on["P"]:
                    p_dve.wait(sp, cp - 1, "comb")
                    st_x1.wait(sp, cp - 1)
                    ld_p.add(sp.dma_start(rn[:, :, :], tokens(xn_d, cp)))
                    ld_p.add(sp.dma_start(x1[:, :, :], tokens(x, cp)))
                if on["Z"]:
                    st_out.wait(sp, cz - 1)
                    st_x1.wait(sp, cz)
                    ld_x1.add(sp.dma_start(x1m[:, :, :], tokens(x1_d, cz)))
                if on["Y"]:
                    y_pool.wait(sp, i - FIRST_Y, "gate")
                    st_y.add(sp.dma_start(tile_of(y_d, i - FIRST_Y), yt[:, :]))
                if on["P"]:
                    if on["Y"]:
                        st_y.wait(sp, i - FIRST_Y)
                    p_dve.wait(sp, cp - 1, "comb")
                    ld_y2.add(sp.dma_start(y2[:, :, :], chunk(y_d, b - 1, j)))
                if on["S"]:
                    st_y.wait(sp, i - FIRST_Y)
                    y_pool.wait(sp, i - FIRST_Y, "gate")
                    ld_yt.add(sp.dma_start(yt[:, :], tile_of(xc_d, i)))
                    ld_yt.add(sp.dma_start(gt[:, :], tile_of(sz_d, i)))
                if on["F"]:
                    f_dve.wait(sp, cf, "xn1")
                    st_xn.add(sp.dma_start(tokens(xn_d, cf), xn[:, :, :]))
                if on["Z"]:
                    z_dve.wait(sp, cz, "out")
                    st_out.add(sp.dma_start(tokens(out, cz), x1m[:, :, :]))
                if on["F"]:
                    f_act.wait(sp, cf, "silu_z")
                    st_sz.add(sp.dma_start(chunk(sz_d, b + 1, j), sz[:, :, :]))
                    f_act.wait(sp, cf, "silu_x")
                    st_xc.add(sp.dma_start(chunk(xc_d, b + 1, j), xc[:, :, :]))
                if on["P"]:
                    p_dve.wait(sp, cp, "x1")
                    st_x1.add(sp.dma_start(tokens(x1_d, cp), x1[:, :, :]))
                if on["F"]:
                    f_act.wait(sp, cf, "xd")
                    st_xd.add(sp.dma_start(
                        bc_d.rearrange("(b r) (j t) -> b j r t", b=BATCH, j=NCH)[b + 1, j], xd[0:2 * NS, :]))
                    if fetch and ends_row:
                        st_xd.wait(sp, cf)
                        load_bc(b + 1, range(NSIG - 1))
                if fetch and not ends_row:
                    load_tile(i + 1, range(NBETA - 1))
                if on["F"]:
                    f_dve.wait(sp, cf, "dt")
                    st_dt.add(sp.dma_start(chunk(dt_d, b + 1, j), dt))
                    f_dve.wait(sp, cf, "dx")
                    st_dx.add(sp.dma_start(chunk(dx_d, b + 1, j), xc[:, :, :]))
                if fetch and ends_row:
                    for st in (st_sz, st_xc, st_dt, st_dx):
                        st.wait(sp, cf)
                    load_tile(i + 1)
                    load_bc(b + 1, range(NSIG - 1, NSIG))
                elif fetch:
                    load_tile(i + 1, range(NBETA - 1, NBETA))

            def whole(b, j0, j1, on):
                if j1 == NCH:
                    j1 -= 1
                    if j1 > j0:
                        whole(b, j0, j1, on)
                    body(b, j1, on, -1 < b < BATCH - 1, True)
                elif j1 - j0 == 1:
                    body(b, j0, on, -1 < b < BATCH, False)
                else:
                    with sp.Fori(j0, j1) as j:
                        body(b, j, on, -1 < b < BATCH, False)

            parts_at = lambda i: next(on for a, e, on in segments() if a <= i < e)
            segs = segments()

            def row(b):
                j = 0
                while j < NCH:
                    i = b * NCH + j
                    seg = next(((a, e, on) for a, e, on in segs if a <= i < e), None)
                    if seg is None:
                        return
                    a, e, on = seg
                    j1 = min(NCH, e - b * NCH)
                    whole(b, j, j1, on)
                    j = j1

            row(-1)
            for st in (st_sz, st_xc, st_xd, st_dt, st_dx):
                st.wait(sp, NCH - 1)
            load_bc(0)
            load_tile(0)
            row(0)
            row(1)
            all_parts = parts_at(2 * NCH)
            with sp.Fori(2, BATCH - 1) as b:
                with sp.Fori(0, NCH - 1) as j:
                    body(b, j, all_parts, True, False)
                body(b, NCH - 1, all_parts, True, True)
            row(BATCH - 1)
            row(BATCH)
            row(BATCH + 1)
            for st, n in ((st_xn, NTILE), (st_y, NTILE), (st_x1, NTILE), (st_out, NTILE)):
                st.wait(sp, n - 1)

        def run(eng, body):
            for a, e, on in segments():
                if e - a == 1:
                    body(a, on)
                else:
                    with eng.Fori(a - FIRST_F, e - FIRST_F) as k:
                        body(k, on, FIRST_F)

        @block.tensor
        def _(pe):
            for s in (f_pe, s_pe, p_pe, m_pe_g, m_pe_t, m_pe_d):
                s.credit(pe)
            pe.wait_ge(ld_w, 16 * (len(weights) + 1))
            pe.wait_ge(w_dve, 1)

            def body(k, on, base=0):
                i = k + base
                cf, cp, cm_, cz = i - FIRST_F, i - FIRST_P, i - FIRST_M, i - FIRST_Z

                def gate_up(n):
                    if n == 0:
                        m_in.wait(pe, cm_, "x2m")
                    g = GU[n % 2]
                    m_dve.wait(pe, cm_ if n >= 2 else cm_ - 1, f"f{(n - 2) % STEPS}")
                    b, p = divmod(n, PAIRS)
                    for q in range(KM):
                        mm = pe.matmul(g[:, :], x2m[:, q, b * P:(b + 1) * P], Wgu[:, q, p, :],
                                       start=(q == 0), stop=(q == KM - 1))
                    m_pe_g.done(mm, f"g{n}")

                def turn(c, n):
                    m_dve.wait(pe, c, f"f{n}")
                    m_aT.wait(pe, c if n >= 1 else c - 1, f"aT{(n - 1) % STEPS}")
                    for e in range(2):
                        mm = pe.transpose(TR[:, e * DE:(e + 1) * DE], th[:, TH[n], e * DE:(e + 1) * DE], ident)
                    m_pe_t.done(mm, f"t{n}")

                def down(c, n):
                    b, p = divmod(n, PAIRS)
                    m_aT.wait(pe, c, f"aT{n}")
                    if p == 0:
                        m_my.wait(pe, c if b else c - 1, f"my{(b - 1) % TB}")
                    for e in range(2):
                        mm = pe.matmul(MY[:, b * DM:(b + 1) * DM], aT[:, n % 2, e * DE:(e + 1) * DE],
                                       Wdn[:, 2 * p + e, :], start=(p == 0 and e == 0),
                                       stop=(p == PAIRS - 1 and e == 1))
                    m_pe_d.done(mm, f"d{n}")

                def add_states(tile, s):
                    if s == 0:
                        y_dve.wait(pe, tile - 1, "skip1")
                    s_hc.wait(pe, tile, f"c{(s + 1) * NBETA - 1}")
                    for h in range(2):
                        for beta in range(NBETA):
                            mm = pe.matmul(Y[h][beta * CB:(beta + 1) * CB, :], sel_y,
                                           hs[:, SLOT[s * NBETA + beta], h * 512:(h + 1) * 512],
                                           start=(s == 0), stop=(s == NSIG - 1), tile_position=(0, beta * CB))
                    s_pe.done(mm, f"y{s}")

                def f_turn():
                    f_dve.wait(pe, cf, "xr1")
                    f_act.wait(pe, cf - 1, f"relu{MT - 1}")
                    for q in range(KM):
                        for b in range(TB):
                            mm = pe.transpose(FB[:, q * CH + b * P:q * CH + (b + 1) * P],
                                              xin[:, b, q * P:(q + 1) * P], ident)
                    f_pe.done(mm, "tr")

                def f_in(r):
                    f_act.wait(pe, cf, "xT" if r == 0 else f"e{r - 1}")
                    for m in range(2):
                        for q in range(KM):
                            c0 = (2 * r + m) * P
                            mm = pe.matmul(FB[:, m * CH:(m + 1) * CH], Win[:, q, c0:c0 + P], xT[:, q, :],
                                           start=(q == 0), stop=(q == KM - 1))
                    f_pe.done(mm, f"ip{r}")

                def f_x():
                    f_act.wait(pe, cf, "silu_x")
                    for m in range(MT):
                        mm = pe.matmul(FB[0:2 * NS + 1, 0:CH], Wx[:, m, :], xc[:, m, :],
                                       start=(m == 0), stop=(m == MT - 1))
                    f_pe.done(mm, "xp")

                def f_dt():
                    f_act.wait(pe, cf, "xd")
                    f_pe.done(pe.matmul(FB[:, CH:2 * CH], SelDt[:, :], xd[:, :], start=True, stop=True), "db")

                def p_out():
                    ld_y2.wait(pe, cp)
                    p_act.wait(pe, cp - 1, "sig")
                    for b in range(TB):
                        for m in range(MT):
                            mm = pe.matmul(PBK[:, b * DM:(b + 1) * DM], y2[:, m, b * P:(b + 1) * P], Wout[:, m, :],
                                           start=(m == 0), stop=(m == MT - 1))
                    p_pe.done(mm, "op")

                def p_turn():
                    p_dve.wait(pe, cp, "x21")
                    for q in range(KM):
                        for b in range(TB):
                            mm = pe.transpose(PBK[:, q * CH + b * P:q * CH + (b + 1) * P],
                                              rn[:, b, q * P:(q + 1) * P], ident)
                    p_pe.done(mm, "tr")

                def p_route():
                    p_act.wait(pe, cp, "x2T")
                    for b in range(TB):
                        for q in range(KM):
                            mm = pe.matmul(PBK[:, b * NE:(b + 1) * NE], x2T[:, q, b * P:(b + 1) * P], Wrt[:, q, :],
                                           start=(q == 0), stop=(q == KM - 1))
                    p_pe.done(mm, "rt")

                at = {}
                if on["F"]:
                    at.update({(3, "F"): [f_turn], (4, "F"): [lambda: f_in(0)], (5, "F"): [lambda: f_in(1)],
                               (6, "F"): [lambda: f_in(2)], (7, "F"): [lambda: f_in(3)],
                               (10, "F"): [f_x], (11, "F"): [f_dt]})
                if on["P"]:
                    at.update({(5, "P"): [p_out], (11, "P"): [p_turn], (12, "P"): [p_route]})
                for n in range(STEPS):
                    if on["M"]:
                        gate_up(n)
                    for f in at.get((n, "F"), []) + at.get((n, "P"), []):
                        f()
                    for lag, step in ((2, turn), (3, down)):
                        if on["M"] and n >= lag:
                            step(cm_, n - lag)
                        if on["Z"] and n < lag:
                            step(cz, n - lag + STEPS)
                    if on["Y"] and n == 0:
                        add_states(i - FIRST_Y, NSIG - 1)
                    if on["S"] and n and n % NBETA == 0:
                        add_states(i, n // NBETA - 1)

            run(pe, body)

        @block.scalar
        def _(act):
            for s in (f_act, s_act, p_act, m_in, m_th, m_aT, m_my):
                s.credit(act)
            act.wait_ge(ld_w, 16 * (len(weights) + 1))
            act.activation(ADall[:, :, 0:UNITS], ADall[:, :, 0:UNITS], ACT.Exp).then_inc(w_act, 1)
            act.wait_ge(w_dve, 2)

            def body(k, on, base=0):
                i = k + base
                cf, cp, cm_, cz = i - FIRST_F, i - FIRST_P, i - FIRST_M, i - FIRST_Z

                def decay(n):
                    beta = n % NBETA
                    if n == 0:
                        s_act.wait(act, i - 1, f"dA{UNITS - 1}")
                        s_act.done(act.activation(Acur[:, :], ADall[:, i % MT, 0:UNITS], ACT.Copy), "ad")
                        s_act.wait(act, i, "ad")
                    if n < NBETA:
                        ld_dt[beta].wait(act, i)
                    s_sc.wait(act, i if n >= NA else i - 1, f"h{(n - NA) % UNITS}")
                    s_act.done(act.activation(dA[:, n % NA, :], dtr[:, beta, :], ACT.Exp, scale=Acur[:, n:n + 1]),
                               f"dA{n}")

                def tanh(n):
                    m_pe_g.wait(act, cm_, f"g{n}")
                    back, m = user_before(TH, n)
                    m_pe_t.wait(act, cm_ + back, f"t{m}")
                    m_th.done(act.activation(th[:, TH[n], :], GU[n % 2][:, 0:2 * DE], ACT.Tanh, scale=0.5), f"th{n}")

                def evac(c, n):
                    m_pe_t.wait(act, c, f"t{n}")
                    m_pe_d.wait(act, c if n >= 2 else c - 1, f"d{(n - 2) % STEPS}")
                    m_aT.done(act.activation(aT[:, n % 2, :], TR[:, 0:2 * DE], ACT.Copy), f"aT{n}")

                def evac_y(c, b):
                    m_pe_d.wait(act, c, f"d{(b + 1) * PAIRS - 1}")
                    z_dve.wait(act, c - 1, "o1")
                    m_my.done(act.activation(my[:, b, :], MY[:, b * DM:(b + 1) * DM], ACT.Copy), f"my{b}")

                def f_xT():
                    f_pe.wait(act, cf, "tr")
                    f_pe.wait(act, cf - 1, "ip3")
                    f_act.done(act.activation(xT[:, :, :], FB[:, :].rearrange("p (q t) -> p q t", q=KM), ACT.Copy), "xT")

                def f_ev(r):
                    f_pe.wait(act, cf, f"ip{r}")
                    src = FB[:, :].rearrange("p (m t) -> p m t", m=2)
                    if r < 2:
                        if r == 0:
                            f_dve.wait(act, cf - 1, "dx")
                            st_dt.wait(act, cf - 1)
                        dst = xb[:, 2 * r:2 * r + 2, HIST:HIST + CH]
                    else:
                        if r == 2:
                            st_xn.wait(act, cf)
                        dst = sz[:, 2 * r - 4:2 * r - 2, :]
                    f_act.done(act.activation(dst, src, ACT.Copy), f"e{r}")

                def f_silu():
                    f_act.wait(act, cf, "e3")
                    f_act.done(act.activation(sz[:, :, :], sz[:, :, :], ACT.Silu), "silu_z")
                    f_dve.wait(act, cf, f"c3{MT - 1}")
                    f_act.done(act.activation(xc[:, :, :], xc[:, :, :], ACT.Silu), "silu_x")

                def f_xd():
                    f_pe.wait(act, cf, "xp")
                    st_xd.wait(act, cf - 1)
                    f_act.done(act.activation(xd[:, :], FB[0:2 * NS + 1, 0:CH], ACT.Copy), "xd")

                def f_sp():
                    f_pe.wait(act, cf, "db")
                    st_sz.wait(act, cf)
                    f_dve.wait(act, cf, "hist")
                    for m in range(MT):
                        wb = dict(scale=dt_w[:, m:m + 1], bias=dt_b[:, m:m + 1])
                        f_act.done(act.activation(sz[:, m, :], FB[:, CH:2 * CH], ACT.Abs, **wb), f"abs{m}")
                        f_act.done(act.activation(dt[:, m, :], FB[:, CH:2 * CH], ACT.Relu, **wb), f"relu{m}")
                    f_act.wait(act, cf, f"abs{MT - 1}")
                    f_act.done(act.activation(sz[:, :, :], sz[:, :, :], ACT.Exp, scale=-1.0), "exp")

                def f_ln():
                    f_dve.wait(act, cf, "lost")
                    f_act.done(act.activation(sz[:, :, :], sz[:, :, :], ACT.Ln, bias=1.0), "ln")

                def p_x2T():
                    p_pe.wait(act, cp, "tr")
                    m_in.wait(act, cp - 1, "x2m")
                    p_act.done(act.activation(x2T[:, :, :], PBK[:, :].rearrange("p (q t) -> p q t", q=KM), ACT.Copy), "x2T")

                def p_sig():
                    p_pe.wait(act, cp, "rt")
                    p_dve.wait(act, cp - 1, "comb")
                    p_act.done(act.activation(R[:, 0, :], PBK[:, 0:TB * NE], ACT.Sigmoid), "sig")

                def take_x():
                    m_pe_g.wait(act, cm_ - 1, f"g{STEPS - 1}")
                    p_act.wait(act, cm_, "x2T")
                    m_in.done(act.activation(x2m[:, :, :], x2T[:, :, :], ACT.Copy), "x2m")

                def take_c():
                    m_dve.wait(act, cm_ - 1, f"f{STEPS - 1}")
                    p_dve.wait(act, cm_, "comb")
                    m_in.done(act.activation(cm[:, :], comb[:, :], ACT.Copy), "cm")

                for n in range(STEPS):
                    if on["M"] and n == 0:
                        take_x()
                    if on["S"]:
                        if n == 0:
                            decay(0)
                        if n + 1 < UNITS:
                            decay(n + 1)
                    if on["M"] and n == 0:
                        take_c()
                    if on["M"]:
                        tanh(n)
                        if n >= 2:
                            evac(cm_, n - 2)
                        if n == PAIRS + 2:
                            evac_y(cm_, 0)
                    if on["Z"]:
                        if n < 2:
                            evac(cz, n - 2 + STEPS)
                        if n == 2:
                            evac_y(cz, 1)
                    if on["F"]:
                        if n == 3:
                            f_xT()
                        if 4 <= n < 8:
                            f_ev(n - 4)
                        if n == 9:
                            f_silu()
                        if n == 10:
                            f_xd()
                        if n == 11:
                            f_sp()
                        if n == 13:
                            f_ln()
                    if on["P"]:
                        if n == 11:
                            p_x2T()
                        if n == 12:
                            p_sig()
            run(act, body)

        @block.gpsimd
        def _(pool):
            for s in (s_up, s_hc, y_pool, f_pool):
                s.credit(pool)

            def body(k, on, base=0):
                i = k + base
                cf = i - FIRST_F

                def inputs(n):
                    s, beta = divmod(n, NBETA)
                    if s == 0:
                        ld_dt[beta].wait(pool, i)
                    ld_bc[s].wait(pool, i // NCH)
                    back, m = user_before(SLOT, n)
                    s_pe.wait(pool, i + back, f"y{m // NBETA}")
                    s_up.done(pool.tensor_tensor(hs[:, SLOT[n], :], dxr[:, beta, :], Bb[:, s, :], ALU.mult), f"u{n}")

                for n in range(UNITS):
                    if on["S"]:
                        for m in range(0 if n == 0 else n + 2, min(n + 3, UNITS)):
                            if m % NBETA in POOL_BETAS:
                                inputs(m)
                    if on["F"] and n == 14:
                        f_act.wait(pool, cf, "ln")
                        f_pool.done(pool.tensor_tensor(low, low, sz[:, :, :], ALU.add), "ln")
                    if on["Y"] and n == 2:
                        y_dve.wait(pool, i - FIRST_Y, "skip1")
                        y_pool.done(pool.tensor_tensor(yt[:, :], yt[:, :], gt[:, :], ALU.mult), "gate")
                    if on["S"]:
                        s_sc.wait(pool, i, f"h{n}")
                        if n % NBETA == 0:
                            ld_bc[n // NBETA].wait(pool, i // NCH)
                        h = hs[:, SLOT[n], :]
                        s_hc.done(pool.tensor_tensor(h, h, Cb[:, n // NBETA, :], ALU.mult), f"c{n}")

            run(pool, body)

        @block.vector
        def _(dve):
            for s in (f_dve, s_u, s_sc, y_dve, p_dve, m_dve, z_dve):
                s.credit(dve)
            dve.wait_ge(ld_w, 16 * (len(weights) + 1))
            for q in range(KM):
                ins = dve.tensor_scalar(Win[:, q, :], Win[:, q, :], norm_w[:, q:q + 1], None, ALU.mult)
            ins.then_inc(w_dve, 1)
            dve.wait_ge(w_act, 1)
            dve.tensor_scalar(ADall[:, :, 0:UNITS], ADall[:, :, 0:UNITS], -1.0, None, ALU.mult).then_inc(w_dve, 1)
            dve.memset(xb[:, :, :], 0.0).then_inc(w_dve, 1)
            dve.wait_ge(w_dve, 3)

            def body(k, on, base=0):
                i = k + base
                cf, cp, cm_, cz, iy = i - FIRST_F, i - FIRST_P, i - FIRST_M, i - FIRST_Z, i - FIRST_Y

                def op(steps, it, name, emit, *after):
                    for a in after[-1:]:
                        steps.wait(dve, it, a)
                    steps.done(emit(), name)

                def rsqrt(steps, it, tag, w, after):
                    v, y, a = w[:, 0, :], w[:, 1, :], w[:, 2, :]
                    op(steps, it, f"{tag}_half", lambda: dve.tensor_scalar(
                        a.bitcast(I32), v.bitcast(I32), 1, None, ALU.logical_shift_right), after)
                    yield
                    op(steps, it, f"{tag}_guess", lambda: dve.tensor_scalar(
                        y.bitcast(I32), a.bitcast(I32), -1.0, RSQRT_MAGIC, ALU.mult, ALU.add), f"{tag}_half")
                    yield
                    last = f"{tag}_guess"
                    for n in range(3):
                        op(steps, it, f"{tag}_a{n}", lambda: dve.scalar_tensor_tensor(
                            out=a, in0=y, scalar=-0.5, in1=y, op0=ALU.mult, op1=ALU.mult), last)
                        yield
                        op(steps, it, f"{tag}_b{n}", lambda: dve.tensor_tensor(a, a, v, ALU.mult), f"{tag}_a{n}")
                        yield
                        op(steps, it, f"{tag}_y{n}", lambda: dve.scalar_tensor_tensor(
                            out=y, in0=a, scalar=1.5, in1=y, op0=ALU.add, op1=ALU.mult), f"{tag}_b{n}")
                        last = f"{tag}_y{n}"
                        yield

                def stats(steps, it, pre, src, st, mv, after):
                    for b in range(TB):
                        op(steps, it, f"{pre}bn{b}", lambda: dve.bn_stats(st[:, b, :], src[:, b, :]), *after)
                        yield
                    op(steps, it, f"{pre}both", lambda: dve.memset(mark[:, :], 0.0), f"{pre}bn1")
                    for b in range(TB):
                        op(steps, it, f"{pre}ag{b}", lambda: dve.bn_aggr(mv[:, b, :], st[:, b, :]))
                        yield

                def part_f():
                    ld_xin.wait(dve, cf)
                    yield from stats(f_dve, cf, "", xin, f_st, f_mv, ())
                    op(f_dve, cf, "w1", lambda: dve.tensor_scalar(f_w[:, 0, 0:TB], f_mv[:, :, 1], LN_EPS, None, ALU.add), "ag1")
                    yield
                    op(f_dve, cf, "w2", lambda: dve.tensor_scalar(
                        f_w[:, 0, TB:2 * TB], f_mv[:, :, 1], 1.0 + RMS_EPS, LN_EPS * RMS_EPS, ALU.mult, ALU.add))
                    yield
                    yield from rsqrt(f_dve, cf, "r", f_w, "w2")
                    f_pool.wait(dve, cf - 1, "ln")
                    for b in range(TB):
                        op(f_dve, cf, f"xn{b}", lambda: dve.tensor_scalar(
                            xn[:, b, :], xin[:, b, :], f_mv[:, b, 0:1], f_w[:, 1, b:b + 1], ALU.subtract, ALU.mult), "r_y2")
                        yield
                    for b in range(TB):
                        op(f_dve, cf, f"xr{b}", lambda: dve.tensor_scalar(
                            xin[:, b, :], xin[:, b, :], f_mv[:, b, 0:1], f_w[:, 1, TB + b:TB + b + 1],
                            ALU.subtract, ALU.mult))
                        yield

                def part_f2():
                    st_dx.wait(dve, cf - 1)
                    f_act.wait(dve, cf, "e1")
                    for t in range(TAPS):
                        for m in range(MT):
                            src = xb[:, m, t:t + CH]
                            if t == 0:
                                op(f_dve, cf, f"c{t}{m}", lambda: dve.tensor_scalar(
                                    xc[:, m, :], src, conv_w[:, m, t:t + 1], conv_b[:, m:m + 1], ALU.mult, ALU.add))
                            else:
                                op(f_dve, cf, f"c{t}{m}", lambda: dve.scalar_tensor_tensor(
                                    out=xc[:, m, :], in0=src, scalar=conv_w[:, m, t:t + 1], in1=xc[:, m, :],
                                    op0=ALU.mult, op1=ALU.add), f"c{t - 1}{m}")
                            yield
                    op(f_dve, cf, "hist", lambda: dve.tensor_scalar(
                        xb[:, :, 0:HIST], xb[:, :, CH:CH + HIST], kp[:, 0:1], None, ALU.mult))
                    yield

                def part_f3():
                    f_act.wait(dve, cf, "exp")
                    op(f_dve, cf, "near", lambda: dve.tensor_scalar(low, sz[:, :, :], 1.0, -1.0, ALU.add, ALU.add))
                    yield
                    op(f_dve, cf, "lost", lambda: dve.tensor_tensor(low, sz[:, :, :], low, ALU.subtract), "near")
                    yield
                    f_pool.wait(dve, cf, "ln")
                    op(f_dve, cf, "dt", lambda: dve.tensor_tensor(dt, dt, low, ALU.add))
                    yield
                    st_xc.wait(dve, cf)
                    f_pe.wait(dve, cf, "xp")
                    op(f_dve, cf, "dx", lambda: dve.tensor_tensor(xc[:, :, :], dt, xc[:, :, :], ALU.mult), "dt")
                    yield

                def inputs(n):
                    s, beta = divmod(n, NBETA)
                    if s == 0:
                        ld_dt[beta].wait(dve, i)
                    if beta == 0:
                        ld_bc[s].wait(dve, i // NCH)
                    back, m = user_before(SLOT, n)
                    s_pe.wait(dve, i + back, f"y{m // NBETA}")
                    s_u.done(dve.tensor_tensor(hs[:, SLOT[n], :], dxr[:, beta, :], Bb[:, s, :], ALU.mult), f"u{n}")

                def scan(n):
                    s_act.wait(dve, i, f"dA{n}")
                    of_u(n % NBETA).wait(dve, i, f"u{n}")
                    s_sc.done(dve.tensor_tensor_scan(hs[:, SLOT[n], :], dA[:, n % NA, :], hs[:, SLOT[n], :], 0.0,
                                                     ALU.mult, ALU.add), f"h{n}")

                def part_y():
                    s_pe.wait(dve, iy, f"y{NSIG - 1}")
                    ld_yt.wait(dve, iy)
                    for h in range(2):
                        op(y_dve, iy, f"skip{h}", lambda: dve.scalar_tensor_tensor(
                            out=yt[:, h * 512:(h + 1) * 512], in0=yt[:, h * 512:(h + 1) * 512],
                            scalar=ADall[:, iy % MT, UNITS:UNITS + 1], in1=Y[h][:, :], op0=ALU.mult, op1=ALU.add))
                        yield

                def part_p():
                    p_pe.wait(dve, cp, "op")
                    ld_p.wait(dve, cp)
                    op(p_dve, cp, "r", lambda: dve.tensor_tensor(
                        rn[:, :, :], PBK[:, :].rearrange("p (b h) -> p b h", b=TB), rn[:, :, :], ALU.add))
                    yield
                    yield from stats(p_dve, cp, "", rn, p_st, p_mv, ("r",))
                    op(p_dve, cp, "w1", lambda: dve.tensor_scalar(p_w[:, 0, :], p_mv[:, :, 1], LN_EPS, None, ALU.add), "ag1")
                    yield
                    yield from rsqrt(p_dve, cp, "r", p_w, "w1")
                    for b in range(TB):
                        op(p_dve, cp, f"o{b}", lambda: dve.tensor_scalar(
                            rn[:, b, :], rn[:, b, :], p_mv[:, b, 0:1], p_w[:, 1, b:b + 1], ALU.subtract, ALU.mult), "r_y2")
                        yield
                    op(p_dve, cp, "x1", lambda: dve.tensor_tensor(x1[:, :, :], rn[:, :, :], x1[:, :, :], ALU.add), "o1")
                    yield
                    yield from stats(p_dve, cp, "B", x1, p_st, p_mv, ("x1",))
                    op(p_dve, cp, "Bw1", lambda: dve.tensor_scalar(p_w[:, 0, :], p_mv[:, :, 1], LN_EPS, None, ALU.add), "Bag1")
                    yield
                    yield from rsqrt(p_dve, cp, "q", p_w, "Bw1")
                    for b in range(TB):
                        op(p_dve, cp, f"x2{b}", lambda: dve.tensor_scalar(
                            rn[:, b, :], x1[:, b, :], p_mv[:, b, 0:1], p_w[:, 1, b:b + 1], ALU.subtract, ALU.mult), "q_y2")
                        yield

                def part_p2():
                    p_act.wait(dve, cp, "sig")
                    G = TB * NG
                    score, sfc, tmp, w = (R[:, k, :] for k in (0, 1, 2, 3))
                    q4 = sfc.rearrange("p (g e) -> p g e", e=NE // NG)
                    hi, lo = (R[:, k, 0:2 * G].rearrange("p (g e) -> p g e", e=2) for k in (4, 5))
                    top1, ta, tb, gs, gr = (R[:, 6, k * G:(k + 1) * G] for k in (0, 1, 2, 3, 1))
                    gm = R[:, 7, 0:G]
                    rk = R[:, 8, :]
                    ws, wr = R[:, 9, 0:TB], R[:, 9, TB:2 * TB]
                    gg, ge = (R[:, k, :].rearrange("p (b i j) -> p b i j", b=TB, i=NG) for k in (10, 11))
                    tt = dve.tensor_tensor
                    o = lambda name, emit, *after: op(p_dve, cp, name, emit, *after)
                    o("sfc", lambda: tt(sfc, score, Ebias[:, :], ALU.add)); yield
                    o("hi", lambda: tt(hi, q4[:, :, 0:2], q4[:, :, 2:4], ALU.max), "sfc"); yield
                    o("lo", lambda: tt(lo, q4[:, :, 0:2], q4[:, :, 2:4], ALU.min)); yield
                    o("t1", lambda: tt(top1, hi[:, :, 0], hi[:, :, 1], ALU.max), "lo"); yield
                    o("t2a", lambda: tt(ta, hi[:, :, 0], hi[:, :, 1], ALU.min)); yield
                    o("t2b", lambda: tt(tb, lo[:, :, 0], lo[:, :, 1], ALU.max)); yield
                    o("t2", lambda: tt(tb, ta, tb, ALU.max), "t2b"); yield
                    o("gs", lambda: tt(gs, top1, tb, ALU.add), "t2"); yield
                    gv = gs.rearrange("p (b g) -> p b g", b=TB)
                    g_j = gv.unsqueeze(2).broadcast_to([P, TB, NG, NG])
                    g_i = gv.unsqueeze(3).broadcast_to([P, TB, NG, NG])
                    bg = before_g.rearrange("p (i j) -> p i j", i=NG).unsqueeze(1).broadcast_to([P, TB, NG, NG])
                    o("ggt", lambda: tt(gg, g_j, g_i, ALU.is_gt), "gs"); yield
                    o("geq", lambda: tt(ge, g_j, g_i, ALU.is_equal)); yield
                    o("gq", lambda: tt(ge, ge, bg, ALU.mult), "geq"); yield
                    o("ga", lambda: tt(gg, gg, ge, ALU.add), "gq"); yield
                    o("gr", lambda: dve.tensor_reduce(gr, R[:, 10, :].rearrange("p (g j) -> p g j", j=NG), AX.X, ALU.add), "ga"); yield
                    o("gm", lambda: dve.tensor_scalar(gm, gr, float(TOPG), None, ALU.is_lt), "gr"); yield
                    t4 = tmp.rearrange("p (g e) -> p g e", e=NE // NG)
                    o("tmp", lambda: tt(t4, q4, gm.unsqueeze(2).broadcast_to([P, G, NE // NG]), ALU.mult), "gm"); yield
                    tv = tmp.rearrange("p (b e) -> p b e", b=TB)
                    e_j = tv.unsqueeze(2).broadcast_to([P, TB, NE, NE])
                    e_i = tv.unsqueeze(3).broadcast_to([P, TB, NE, NE])
                    gt_, eq_ = (RR[:, k, :].rearrange("p (b i j) -> p b i j", b=TB, i=NE) for k in (0, 1))
                    be = before.rearrange("p (i j) -> p i j", i=NE).unsqueeze(1).broadcast_to([P, TB, NE, NE])
                    o("gt", lambda: tt(gt_, e_j, e_i, ALU.is_gt), "tmp"); yield
                    o("eq", lambda: tt(eq_, e_j, e_i, ALU.is_equal)); yield
                    o("eqb", lambda: tt(eq_, eq_, be, ALU.mult), "eq"); yield
                    o("ad", lambda: tt(RR[:, 0, :], RR[:, 0, :], RR[:, 1, :], ALU.add), "eqb"); yield
                    o("rk", lambda: dve.tensor_reduce(rk, RR[:, 0, :].rearrange("p (r j) -> p r j", j=NE), AX.X, ALU.add), "ad"); yield
                    o("w", lambda: dve.scalar_tensor_tensor(out=w, in0=rk, scalar=float(TOPK), in1=score,
                                                            op0=ALU.is_lt, op1=ALU.mult), "rk"); yield
                    wv = w.rearrange("p (b e) -> p b e", b=TB)
                    o("ws", lambda: dve.tensor_reduce(ws, wv, AX.X, ALU.add), "w"); yield
                    o("we", lambda: dve.tensor_scalar(ws, ws, 1e-20, None, ALU.add), "ws"); yield
                    o("wr", lambda: dve.reciprocal(wr, ws), "we"); yield
                    m_in.wait(dve, cp - 1, "cm")
                    op(p_dve, cp, "comb", lambda: dve.scalar_tensor_tensor(
                        out=comb[:, :].rearrange("p (b e) -> p b e", b=TB), in0=wv, scalar=0.5,
                        in1=wr.unsqueeze(2).broadcast_to([P, TB, NE]), op0=ALU.mult, op1=ALU.mult), "wr")
                    yield

                def expert(n):
                    b, p = divmod(n, PAIRS)
                    g = GU[n % 2]
                    m_th.wait(dve, cm_, f"th{n}")
                    op(m_dve, cm_, f"a{n}", lambda: dve.scalar_tensor_tensor(
                        out=th[:, TH[n], :], in0=th[:, TH[n], :], scalar=1.0, in1=g[:, 0:2 * DE],
                        op0=ALU.add, op1=ALU.mult))
                    yield
                    if n == 0:
                        m_in.wait(dve, cm_, "cm")
                    for e, name in enumerate("ef"):
                        c = b * NE + 2 * p + e
                        sl = slice(e * DE, (e + 1) * DE)
                        op(m_dve, cm_, f"{name}{n}", lambda: dve.scalar_tensor_tensor(
                            out=th[:, TH[n], sl], in0=g[:, (2 + e) * DE:(3 + e) * DE], scalar=cm[:, c:c + 1],
                            in1=th[:, TH[n], sl], op0=ALU.mult, op1=ALU.mult), f"a{n}")
                        yield

                def part_z():
                    m_my.wait(dve, cz, f"my{TB - 1}")
                    ld_x1.wait(dve, cz)
                    yield from stats(z_dve, cz, "", my, z_st, z_mv, ())
                    op(z_dve, cz, "w1", lambda: dve.tensor_scalar(z_w[:, 0, :], z_mv[:, :, 1], LN_EPS, None, ALU.add), "ag1")
                    yield
                    yield from rsqrt(z_dve, cz, "r", z_w, "w1")
                    for b in range(TB):
                        op(z_dve, cz, f"o{b}", lambda: dve.tensor_scalar(
                            my[:, b, :], my[:, b, :], z_mv[:, b, 0:1], z_w[:, 1, b:b + 1], ALU.subtract, ALU.mult), "r_y2")
                        yield
                    op(z_dve, cz, "out", lambda: dve.tensor_tensor(x1m[:, :, :], my[:, :, :], x1m[:, :, :], ALU.add), "o1")
                    yield

                chains = dict(F1=part_f(), F2=part_f2(), F3=part_f3(), P1=part_p(), P2=part_p2(), Z=part_z(), Y=part_y())

                def shuffle(n):
                    left = {c: k for c, k in PLAN.get(n, {}).items() if on[c[0]]}
                    while left:
                        for c in list(left):
                            if next(chains[c], "end") == "end":
                                del left[c]
                                continue
                            yield
                            left[c] -= 1
                            if not left[c]:
                                del left[c]

                def big(n):
                    if on["S"]:
                        for m in range(0 if n == 0 else n + 1, min(n + 2, UNITS)):
                            if m % NBETA not in POOL_BETAS:
                                inputs(m)
                                yield
                        scan(n)
                        yield
                    if on["M"]:
                        yield from expert(n)

                for n in range(UNITS):
                    small, want = shuffle(n), sum(min(k, 10) for c, k in PLAN.get(n, {}).items() if on[c[0]])
                    slots = (2 if on["S"] else 0) + (3 if on["M"] else 0)
                    each = -(-want // slots) if slots else 0
                    for _ in big(n):
                        for _ in range(each):
                            next(small, None)
                    for _ in small:
                        pass

            run(dve, body)


def kernel(**inputs):
    import concourse.bacc as bacc
    from concourse.bass_utils import run_bass_kernel_spmd

    g = {k.removeprefix("L0_"): np.asarray(v) for k, v in inputs.items()}
    tiles = lambda a: np.ascontiguousarray(a.reshape(-1, P, *a.shape[1:]).swapaxes(0, 1))
    eye = np.eye(P, dtype=np.float32)
    order = list(range(1, 2 * NS + 1)) + [0]
    gate = g["ffn_gate_proj"].transpose(2, 0, 1).reshape(DM, PAIRS, 2 * DE)
    up = g["ffn_up_proj"].transpose(2, 0, 1).reshape(DM, PAIRS, 2 * DE)
    alog = g["attn_A_log"].reshape(MT, NBETA, CB, NSIG, SG).transpose(4, 2, 0, 3, 1).reshape(P, MT, UNITS)
    col = lambda a: tiles(a.reshape(DI, 1))[:, :, 0]
    conv = tiles(g["attn_conv_w"].reshape(DI, TAPS)).reshape(P, MT * TAPS)
    i_, j_ = np.arange(NE), np.arange(NG)
    before = (i_[None, :] < i_[:, None]).astype(np.float32).reshape(1, -1)
    before_g = (j_[None, :] < j_[:, None]).astype(np.float32).reshape(1, -1)
    sel_dt = np.zeros((2 * NS + 1, P), np.float32)
    sel_dt[2 * NS] = 1.0
    keep = np.ones((NCH, P, 1), np.float32)
    keep[NCH - 1] = 0.0
    arrays = dict(
        x=np.ascontiguousarray(g["attn_x"].reshape(BATCH * SEQ, DM)),
        w_in=tiles(g["attn_in_proj_w"]),
        w_out=tiles(g["attn_out_proj_w"]),
        w_gu=tiles(np.concatenate([gate, up], axis=2)),
        w_dn=np.ascontiguousarray(g["ffn_down_proj"].transpose(2, 0, 1)),
        w_x=tiles(g["attn_x_proj_w"][:, order]),
        w_rt=tiles(np.ascontiguousarray(g["ffn_gate_weight"].T)),
        cols=np.concatenate([conv, col(g["attn_conv_b"]), col(g["attn_dt_proj_w"]), col(g["attn_dt_proj_b"]),
                             col(g["attn_D"]), tiles(g["attn_norm_w"].reshape(DM, 1))[:, :, 0]], axis=1),
        alog=np.concatenate([alog, col(g["attn_D"])[:, :, None]], axis=2),
        ebias=np.broadcast_to(np.tile(g["ffn_e_bias"], TB), (P, TB * NE)),
        consts=np.concatenate([eye, np.tile(np.eye(CB, dtype=np.float32), (SG, 1)),
                               np.broadcast_to(before, (P, NE * NE)), np.broadcast_to(before_g, (P, NG * NG))], axis=1),
        sel_dt=sel_dt,
        keep=keep,
    )
    nc = bacc.Bacc("TRN2", target_bir_lowering=False, num_devices=1)
    feed, args = {}, []
    for name, a in arrays.items():
        a = np.ascontiguousarray(a)
        feed[f"in_{name}"] = a
        args.append(nc.dram_tensor(f"in_{name}", a.shape, mybir.dt.from_np(a.dtype), kind="ExternalInput").ap())
    o = nc.dram_tensor("out_0", (BATCH * SEQ, DM), F32, kind="ExternalOutput").ap()
    sandwich_kernel(nc, *args, o)
    r = run_bass_kernel_spmd(nc, [feed], core_ids=[0])
    return r.results[0]["out_0"].reshape(BATCH, SEQ, DM)
```

```python
from contextlib import ExitStack

import numpy as np
import concourse.bass as bass
from concourse import mybir

F32 = mybir.dt.float32
I32 = mybir.dt.int32
ALU = mybir.AluOpType
ACT = mybir.ActivationFunctionType
AX = mybir.AxisListType

P = 128
BATCH, SEQ, DM = 8, 1024, 256
DI, NS, TAPS = 512, 16, 4
NE, NG, DE, TOPK, TOPG = 16, 4, 128, 4, 2
CH = 256
TB = CH // P
KM = DM // P
MT = DI // P
NCH = SEQ // CH
NTILE = BATCH * MT
SG = 4
CB = P // SG
NSIG = NS // SG
NBETA = P // CB
UNITS = NSIG * NBETA
NA, NH, NTH, NUC = 2, 6, 4, 2
SLOT = [0, 1, 2, 3, 4, 5, 0, 1, 2, 3, 0, 1, 4, 5, 2, 3]
POOL_UNITS = (7, 9, 15)
PAIRS = NE // 2
STEPS = TB * PAIRS
HIST = TAPS - 1
assert len(SLOT) == UNITS == STEPS and STEPS % NTH == STEPS % NUC == 0
LN_EPS, RMS_EPS = 1e-5, 1e-6
RSQRT_MAGIC = float(0x5F3759DF)

FIRST_E, FIRST_F, FIRST_S, FIRST_Y, FIRST_P, FIRST_M, FIRST_Z = -NCH - 2, -NCH - 1, 0, 1, NCH, NCH + 1, NCH + 2
PARTS = dict(E=FIRST_E, F=FIRST_F, S=FIRST_S, Y=FIRST_Y, P=FIRST_P, M=FIRST_M, Z=FIRST_Z)


ALL = 99
PLAN = {1: dict(Y=2), 3: dict(F2=5), 4: dict(F2=5, Z=2),
        5: dict(F2=ALL, Z=8), 6: dict(P1=8, Z=ALL), 7: dict(P1=11), 8: dict(P1=11), 9: dict(P1=ALL),
        10: dict(E1=10), 11: dict(E1=ALL, F3=2), 12: dict(P2=4), 13: dict(P2=6, F4=1), 14: dict(P2=7, F4=1),
        15: dict(P2=ALL)}


def segments():
    cuts = sorted({f for f in PARTS.values()} | {f + NTILE for f in PARTS.values()})
    out = []
    for a, b in zip(cuts, cuts[1:]):
        out.append((a, b, {p: f <= a < f + NTILE for p, f in PARTS.items()}))
    return out


def rsqrt_names(tag):
    return [f"{tag}_half", f"{tag}_guess"] + [f"{tag}_{s}{n}" for n in range(3) for s in ("a", "b", "y")]


TICK = {}


def settle(eng):
    if eng is TICK.get("engine"):
        eng.sem_inc(TICK["sem"], 1)


class Steps:

    def __init__(self, sem, names):
        self.sem, self.names, self.per, self.at = sem, names, len(names), 0
        assert len(set(names)) == len(names)

    def credit(self, eng):
        eng.sem_inc(self.sem, self.per)

    def done(self, ins, name):
        assert self.names[self.at % self.per] == name, (name, self.names[self.at % self.per])
        self.at += 1
        ins.then_inc(self.sem, 1)

    def wait(self, eng, it, name):
        eng.wait_ge(self.sem, it * self.per + (self.per + self.names.index(name) + 1))
        settle(eng)


def user_before(slots, n):
    m = n - 1
    while slots[m % len(slots)] != slots[n]:
        m -= 1
    return divmod(m, len(slots))


class Moves:

    def __init__(self, sem, n=1):
        self.sem, self.per = sem, 16 * n

    def credit(self, eng):
        eng.sem_inc(self.sem, self.per)

    def add(self, ins):
        ins.then_inc(self.sem, 16)

    def wait(self, eng, it):
        eng.wait_ge(self.sem, it * self.per + 2 * self.per)
        settle(eng)


def sandwich_kernel(nc, x, w_in, w_out, w_gu, w_dn, w_x, w_rt, cols, alog, ebias, consts, sel_dt, keep, out):
    with ExitStack() as ctx:
        def sb(name, shape, dt=F32):
            return ctx.enter_context(nc.sbuf_tensor(name, shape, dt))

        def pb(name):
            return ctx.enter_context(nc.psum_tensor(name, [P, 512], F32))

        def sem(name):
            return ctx.enter_context(nc.semaphore(name))

        def scratch(name, shape):
            return nc.dram_tensor(name, shape, F32, kind="Internal").ap()

        dt_d = scratch("dt_d", (BATCH * DI, SEQ))
        dx_d = scratch("dx_d", (BATCH * DI, SEQ))
        xc_d = scratch("xc_d", (BATCH * DI, SEQ))
        sz_d = scratch("sz_d", (BATCH * DI, SEQ))
        y_d = scratch("y_d", (BATCH * DI, SEQ))
        bc_d = scratch("bc_d", (BATCH * 2 * NS, SEQ))
        x1_d = scratch("x1_d", (BATCH * SEQ, DM))

        def tokens(t, c):
            return t.rearrange("(c b p) h -> c p b h", b=TB, p=P)[c]

        def chunk(t, b, j):
            return t.rearrange("(b m p) (j t) -> b j p m t", m=MT, p=P, j=NCH)[b, j]

        def tile_of(t, i):
            return t.rearrange("(i p) t -> i p t", p=P)[i]

        Win = sb("Win", [P, KM, 2 * DI])
        Wout = sb("Wout", [P, MT, DM])
        Wgu = sb("Wgu", [P, KM, PAIRS, 4 * DE])
        Wdn = sb("Wdn", [P, NE, DM])
        Wx = sb("Wx", [P, MT, 2 * NS + 1])
        Wrt = sb("Wrt", [P, KM, NE])
        Cols = sb("Cols", [P, MT * (TAPS + 4) + KM])
        ADall = sb("ADall", [P, MT, UNITS + 1])
        Acur = sb("Acur", [P, UNITS])
        Ebias = sb("Ebias", [P, TB * NE])
        Cst = sb("Cst", [P, P + CB + NE * NE + NG * NG])
        SelDt = sb("SelDt", [2 * NS + 1, P])
        conv_w = Cols[:, 0:MT * TAPS].rearrange("p (m k) -> p m k", m=MT)
        conv_b, dt_w, dt_b, d_col = (Cols[:, MT * (TAPS + k):MT * (TAPS + k + 1)] for k in range(4))
        norm_w = Cols[:, MT * (TAPS + 4):MT * (TAPS + 4) + KM]
        ident = Cst[:, 0:P]
        sel_y = Cst[:, P:P + CB]
        before = Cst[:, P + CB:P + CB + NE * NE]
        before_g = Cst[:, P + CB + NE * NE:P + CB + NE * NE + NG * NG]

        xin = sb("xin", [P, TB, DM])
        fx = sb("fx", [P, 2 * TB * DM])
        xT = fx[:, TB * DM:].rearrange("p (q t) -> p q t", q=KM)
        low = fx[:, :].rearrange("p (m t) -> p m t", m=MT)
        xb = sb("xb", [P, MT, HIST + CH])
        xc = sb("xc", [P, MT, CH])
        sz = sb("sz", [P, MT, CH])
        ln1 = sb("ln1", [P, NTILE, 2 * TB])
        dt = xb[:, :, HIST:HIST + CH]
        xd = sb("xd", [2 * NS + 1, CH])
        kp = sb("kp", [P, 1])
        f_st = sb("f_st", [P, TB, 6])
        f_mv = sb("f_mv", [P, TB, 2])
        f_w = sb("f_w", [P, 3, 2 * TB])
        mark = sb("mark", [P, 1])
        dtr = sb("dtr", [P, NBETA, SEQ])
        dxr = sb("dxr", [P, NBETA, SEQ])
        Bb = sb("Bb", [P, NSIG, SEQ])
        Cb = sb("Cb", [P, NSIG, SEQ])
        dA = sb("dA", [P, NA, SEQ])
        hs = sb("hs", [P, NH, SEQ])
        yt = sb("yt", [P, SEQ])
        y2 = sb("y2", [P, MT, CH])
        gt = y2[:, :, :].rearrange("p m t -> p (m t)")
        assert MT * CH == SEQ
        rn = sb("rn", [P, TB, DM])
        x1 = fx[:, 0:TB * DM].rearrange("p (b h) -> p b h", b=TB)
        x2T = sb("x2T", [P, KM, CH])
        p_st = sb("p_st", [P, TB, 6])
        p_mv = sb("p_mv", [P, TB, 2])
        p_w = sb("p_w", [P, 3, TB])
        R = rn[:, :, :].rearrange("p b h -> p (b h)")[:, 0:12 * TB * NE].rearrange("p (k e) -> p k e", k=12)
        assert MT * CH == 2 * TB * NE * NE
        RR = y2[:, :, :].rearrange("p (k m) t -> p k (m t)", k=2)
        comb = sb("comb", [P, TB * NE])
        x2m = sb("x2m", [P, KM, CH])
        cm = sb("cm", [P, TB * NE])
        th = sb("th", [P, NTH, 2 * DE])
        uc = sb("uc", [P, NUC, 2 * DE])
        aT = sb("aT", [P, 2, 2 * DE])
        my = sb("my", [P, TB, DM])
        x1m = sb("x1m", [P, TB, DM])
        z_st = sb("z_st", [P, TB, 6])
        z_mv = sb("z_mv", [P, TB, 2])
        z_w = sb("z_w", [P, 3, TB])

        Y = [pb("Y0"), pb("Y1")]
        GU = [pb("GU0"), pb("GU1")]
        TR, MY, FB, PBK = pb("TR"), pb("MY"), pb("FB"), pb("PBK")

        e_dve = Steps(sem("e_dve"), ["bn0", "bn1", "both", "ag0", "ag1", "w1", "w2"] + rsqrt_names("r")
                      + ["mean", "dev", "xr0", "xr1"])
        f_dve = Steps(sem("f_dve"), [f"c{k}{m}" for k in range(TAPS) for m in range(MT)]
                      + ["hist", "near", "lost", "dt", "dx"])
        f_pool = Steps(sem("f_pool"), ["ln"])
        f_pe = Steps(sem("f_pe"), ["tr", "ip0", "ip1", "ip2", "ip3", "xp", "db"])
        f_act = Steps(sem("f_act"), ["xT", "e0", "e1", "e2", "e3", "silu_z", "silu_x", "xd"]
                      + [f"{k}{m}" for m in range(MT) for k in ("abs", "relu")] + ["exp", "ln"])
        s_act = Steps(sem("s_act"), ["ad"] + [f"dA{n}" for n in range(UNITS)])
        s_u = Steps(sem("s_u"), [f"u{n}" for n in range(UNITS) if n not in POOL_UNITS])
        s_up = Steps(sem("s_up"), [f"u{n}" for n in range(UNITS) if n in POOL_UNITS])
        s_sc = Steps(sem("s_sc"), [f"h{n}" for n in range(UNITS)])
        s_hc = Steps(sem("s_hc"), [f"c{n}" for n in range(UNITS)])
        s_pe = Steps(sem("s_pe"), [f"y{s}" for s in range(NSIG)])
        y_dve = Steps(sem("y_dve"), ["skip0", "skip1"])
        y_pool = Steps(sem("y_pool"), ["gate"])
        route = (["sfc", "hi", "lo", "t1", "t2a", "t2b", "t2", "gs", "ggt", "geq", "gq", "ga", "gr", "gm",
                  "tmp", "gt", "eq", "eqb", "ad", "rk", "w", "ws", "we", "wr", "comb"])
        p_dve = Steps(sem("p_dve"), ["xn0", "xn1", "r", "bn0", "bn1", "both", "ag0", "ag1", "w1"] + rsqrt_names("r") + ["o0", "o1", "x1"]
                      + ["Bbn0", "Bbn1", "Bboth", "Bag0", "Bag1", "Bw1"] + rsqrt_names("q") + ["x20", "x21"] + route)
        p_pe = Steps(sem("p_pe"), ["op0", "op1", "tr", "rt"])
        p_act = Steps(sem("p_act"), ["x2T", "sig"])
        m_in = Steps(sem("m_in"), ["x2m", "cm"])
        m_pe_g = Steps(sem("m_pe_g"), [f"g{n}" for n in range(STEPS)])
        m_pe_t = Steps(sem("m_pe_t"), [f"t{n}" for n in range(STEPS)])
        m_pe_d = Steps(sem("m_pe_d"), [f"d{n}" for n in range(STEPS)])
        m_th = Steps(sem("m_th"), [f"th{n}" for n in range(STEPS)])
        m_aT = Steps(sem("m_aT"), [f"aT{n}" for n in range(STEPS)])
        m_my = Steps(sem("m_my"), [f"my{b}" for b in range(TB)])
        m_uc = Steps(sem("m_uc"), [f"uc{n}" for n in range(STEPS)])
        m_dve = Steps(sem("m_dve"), [f"a{n}" for n in range(STEPS)])
        m_pool = Steps(sem("m_pool"), [f"f{n}" for n in range(STEPS)])
        z_dve = Steps(sem("z_dve"), ["bn0", "bn1", "both", "ag0", "ag1", "w1"] + rsqrt_names("r") + ["o0", "o1", "out"])

        ld_w, ld_w2 = sem("ld_w"), sem("ld_w2")
        w_act, w_dve = sem("w_act"), sem("w_dve")
        ld_xin, ld_kp = Moves(sem("ld_xin")), Moves(sem("ld_kp"))
        ld_dt = [Moves(sem(f"ld_dt{b}"), 2) for b in range(NBETA)]
        ld_bc = [Moves(sem(f"ld_bc{s}"), 2) for s in range(NSIG)]
        ld_yt, ld_gt, ld_y2, ld_p, ld_x1 = Moves(sem("ld_yt")), Moves(sem("ld_gt")), Moves(sem("ld_y2")), Moves(sem("ld_p")), Moves(sem("ld_x1"))
        st_sz, st_xc, st_xd, st_dt, st_dx = (Moves(sem(f"st_{k}")) for k in ("sz", "xc", "xd", "dt", "dx"))
        st_y, st_x1, st_out = (Moves(sem(f"st_{k}")) for k in ("y", "x1", "out"))

        def of_u(n):
            return s_up if n in POOL_UNITS else s_u

        block = ctx.enter_context(nc.Block())

        early = [(ADall, alog), (Cst, consts), (Cols, cols), (Win, w_in), (Wx, w_x), (SelDt, sel_dt)]
        late = [[(Wout, w_out), (Wrt, w_rt), (Ebias, ebias), (Wgu[:, 0], w_gu[:, 0])], [(Wgu[:, 1], w_gu[:, 1])],
                [(Wdn, w_dn)]]
        assert KM == 2

        @block.sync
        def _(sp):
            TICK.update(engine=sp, sem=sem("sp_tick"))
            for m in (ld_xin, ld_kp, *ld_dt, *ld_bc, ld_yt, ld_gt, ld_y2, ld_p, ld_x1,
                      st_sz, st_xc, st_xd, st_dt, st_dx, st_y, st_x1, st_out):
                m.credit(sp)

            def load_weights(lot, done):
                for t, src in lot:
                    sp.dma_start(t[tuple(slice(None) for _ in src.shape)], src).then_inc(done, 16)

            load_weights(early, ld_w)

            def load_tile(i, betas=range(NBETA)):
                for beta in betas:
                    rows = slice(beta * CB, (beta + 1) * CB)
                    s_act.wait(sp, i - 1, f"dA{UNITS - NBETA + beta}")
                    ld_dt[beta].add(sp.dma_start(dtr[:, beta, :], tile_of(dt_d, i)[rows, :].partition_broadcast(SG)))
                    of_u(UNITS - NBETA + beta).wait(sp, i - 1, f"u{UNITS - NBETA + beta}")
                    ld_dt[beta].add(sp.dma_start(dxr[:, beta, :], tile_of(dx_d, i)[rows, :].partition_broadcast(SG)))

            def load_bc(b, sigmas=range(NSIG)):
                last = b * NCH - 1
                for s in sigmas:
                    end = (s + 1) * NBETA - 1
                    for k, t in enumerate((Bb, Cb)):
                        if k == 0:
                            for steps in (s_u, s_up):
                                for u in [u for u in steps.names if int(u[1:]) <= end][-1:]:
                                    steps.wait(sp, last, u)
                        else:
                            s_hc.wait(sp, last, f"c{end}")
                        src = bc_d.rearrange("(b k s g) t -> b k s g t", b=BATCH, k=2, g=SG)[b, k, s]
                        ld_bc[s].add(sp.dma_start(t[:, s, :], src.unsqueeze(1).broadcast_to([SG, CB, SEQ])))

            def body(b, j, on, fetch, ends_row):
                i = b * NCH + j
                ce, cf, cp, cz = i - FIRST_E, i - FIRST_F, i - FIRST_P, i - FIRST_Z
                fb, fj = (b + 2, 0) if ends_row else (b + 1, j + 1)
                if on["Y"]:
                    if on["P"]:
                        p_dve.wait(sp, cp - 1, "comb")
                    y_pool.wait(sp, i - FIRST_Y - 1, "gate")
                    ld_gt.add(sp.dma_start(gt, tile_of(sz_d, i - FIRST_Y)))
                if on["P"]:
                    st_x1.wait(sp, cp - 1)
                    p_dve.wait(sp, cp - 1, "x21")
                    f_dve.wait(sp, cf - 1 if on["F"] else NTILE - 1, "dt")
                    ld_p.add(sp.dma_start(x1, tokens(x, cp)))
                if on["Z"]:
                    st_out.wait(sp, cz - 1)
                    st_x1.wait(sp, cz)
                    ld_x1.add(sp.dma_start(x1m[:, :, :], tokens(x1_d, cz)))
                if on["F"]:
                    f_dve.wait(sp, cf - 1, "hist")
                    ld_kp.add(sp.dma_start(kp[:, :], keep[fj]))
                if on["E"]:
                    f_pe.wait(sp, ce - 1, "tr")
                    ld_xin.add(sp.dma_start(xin[:, :, :], tokens(x, ce)))
                if on["Y"]:
                    y_pool.wait(sp, i - FIRST_Y, "gate")
                    st_y.add(sp.dma_start(tile_of(y_d, i - FIRST_Y), yt[:, :]))
                if on["P"]:
                    st_y.wait(sp, i - FIRST_Y if on["Y"] else NTILE - 1)
                    y_pool.wait(sp, i - FIRST_Y if on["Y"] else NTILE - 1, "gate")
                    p_dve.wait(sp, cp - 1, "comb")
                    ld_y2.add(sp.dma_start(y2[:, :, :], chunk(y_d, b - 1, j)))
                if on["S"]:
                    st_y.wait(sp, i - FIRST_Y)
                    y_pool.wait(sp, i - FIRST_Y, "gate")
                    for st in (st_xc, st_sz):
                        st.wait(sp, b * NCH + NCH - 1)
                    ld_yt.add(sp.dma_start(yt[:, :], tile_of(xc_d, i)))
                if on["Z"]:
                    z_dve.wait(sp, cz, "out")
                    st_out.add(sp.dma_start(tokens(out, cz), x1m[:, :, :]))
                if on["P"]:
                    p_dve.wait(sp, cp, "x1")
                    st_x1.add(sp.dma_start(tokens(x1_d, cp), x1))
                if on["F"]:
                    f_act.wait(sp, cf, "silu_z")
                    st_sz.add(sp.dma_start(chunk(sz_d, fb, fj), sz[:, :, :]))
                    f_act.wait(sp, cf, "silu_x")
                    st_xc.add(sp.dma_start(chunk(xc_d, fb, fj), xc[:, :, :]))
                    f_act.wait(sp, cf, "xd")
                    st_xd.add(sp.dma_start(
                        bc_d.rearrange("(b r) (j t) -> b j r t", b=BATCH, j=NCH)[fb, fj], xd[0:2 * NS, :]))
                if fetch and ends_row:
                    for st in (st_xd, st_dt, st_dx):
                        st.wait(sp, b * NCH + 2 * NCH - 1)
                    load_bc(b + 1, range(NSIG - 1))
                if fetch:
                    load_tile(i + 1, range(NBETA // 2))
                if on["F"]:
                    f_dve.wait(sp, cf, "dt")
                    st_dt.add(sp.dma_start(chunk(dt_d, fb, fj), dt))
                if fetch:
                    load_tile(i + 1, range(NBETA // 2, NBETA - 1))
                if on["F"]:
                    f_dve.wait(sp, cf, "dx")
                    st_dx.add(sp.dma_start(chunk(dx_d, fb, fj), xc[:, :, :]))
                if fetch:
                    load_tile(i + 1, range(NBETA - 1, NBETA))
                    if ends_row:
                        load_bc(b + 1, range(NSIG - 1, NSIG))

            def whole(b, j0, j1, on):
                if j1 == NCH:
                    j1 -= 1
                    if j1 > j0:
                        whole(b, j0, j1, on)
                    body(b, j1, on, -1 < b < BATCH - 1, True)
                elif j1 - j0 == 1:
                    body(b, j0, on, -1 < b < BATCH, False)
                else:
                    with sp.Fori(j0, j1) as j:
                        body(b, j, on, -1 < b < BATCH, False)

            parts_at = lambda i: next(on for a, e, on in segments() if a <= i < e)
            segs = segments()

            def row(b):
                j = 0
                while j < NCH:
                    i = b * NCH + j
                    seg = next(((a, e, on) for a, e, on in segs if a <= i < e), None)
                    if seg is None:
                        return
                    a, e, on = seg
                    j1 = min(NCH, e - b * NCH)
                    whole(b, j, j1, on)
                    j = j1

            body(-2, NCH - 2, parts_at(FIRST_E), False, False)
            body(-2, NCH - 1, parts_at(FIRST_F), False, True)
            load_weights(late[0], ld_w2)
            for j in range(NCH):
                body(-1, j, parts_at(j - NCH), False, j == NCH - 1)
                if j + 1 < len(late):
                    load_weights(late[j + 1], ld_w2)
            for st in (st_xd, st_dt, st_dx):
                st.wait(sp, NCH - 1)
            load_bc(0)
            load_tile(0)
            row(0)
            row(1)
            all_parts = parts_at(2 * NCH)
            with sp.Fori(2, BATCH - 2) as b:
                with sp.Fori(0, NCH - 1) as j:
                    body(b, j, all_parts, True, False)
                body(b, NCH - 1, all_parts, True, True)
            row(BATCH - 2)
            row(BATCH - 1)
            row(BATCH)
            row(BATCH + 1)
            for st, n in ((st_y, NTILE), (st_x1, NTILE), (st_out, NTILE)):
                st.wait(sp, n - 1)

        def run(eng, body):
            for a, e, on in segments():
                if a == FIRST_P:
                    eng.wait_ge(ld_w2, 16 * sum(len(lot) for lot in late))
                if e - a == 1:
                    body(a, on)
                else:
                    with eng.Fori(a - FIRST_E, e - FIRST_E) as k:
                        body(k, on, FIRST_E)

        @block.tensor
        def _(pe):
            for s in (f_pe, s_pe, p_pe, m_pe_g, m_pe_t, m_pe_d):
                s.credit(pe)
            pe.wait_ge(ld_w, 16 * len(early))
            pe.wait_ge(w_dve, 1)

            def body(k, on, base=0):
                i = k + base
                cf, cp, cm_, cz = i - FIRST_F, i - FIRST_P, i - FIRST_M, i - FIRST_Z

                def gate_up(n):
                    if n == 0:
                        m_in.wait(pe, cm_, "x2m")
                    g = GU[n % 2]
                    c = cm_ if n >= 2 else cm_ - 1
                    m_dve.wait(pe, c, f"a{(n - 2) % STEPS}")
                    m_uc.wait(pe, c, f"uc{(n - 2) % STEPS}")
                    b, p = divmod(n, PAIRS)
                    for q in range(KM):
                        mm = pe.matmul(g[:, :], x2m[:, q, b * P:(b + 1) * P], Wgu[:, q, p, :],
                                       start=(q == 0), stop=(q == KM - 1))
                    m_pe_g.done(mm, f"g{n}")

                def turn(c, n):
                    m_pool.wait(pe, c, f"f{n}")
                    m_aT.wait(pe, c if n >= 1 else c - 1, f"aT{(n - 1) % STEPS}")
                    for e in range(2):
                        mm = pe.transpose(TR[:, e * DE:(e + 1) * DE], th[:, n % NTH, e * DE:(e + 1) * DE], ident)
                    m_pe_t.done(mm, f"t{n}")

                def down(c, n):
                    b, p = divmod(n, PAIRS)
                    m_aT.wait(pe, c, f"aT{n}")
                    if p == 0:
                        m_my.wait(pe, c if b else c - 1, f"my{(b - 1) % TB}")
                    for e in range(2):
                        mm = pe.matmul(MY[:, b * DM:(b + 1) * DM], aT[:, n % 2, e * DE:(e + 1) * DE],
                                       Wdn[:, 2 * p + e, :], start=(p == 0 and e == 0),
                                       stop=(p == PAIRS - 1 and e == 1))
                    m_pe_d.done(mm, f"d{n}")

                def add_states(tile, s):
                    if s == 0:
                        y_dve.wait(pe, tile - 1, "skip1")
                    s_hc.wait(pe, tile, f"c{(s + 1) * NBETA - 1}")
                    for h in range(2):
                        for beta in range(NBETA):
                            mm = pe.matmul(Y[h][beta * CB:(beta + 1) * CB, :], sel_y,
                                           hs[:, SLOT[s * NBETA + beta], h * 512:(h + 1) * 512],
                                           start=(s == 0), stop=(s == NSIG - 1), tile_position=(0, beta * CB))
                    s_pe.done(mm, f"y{s}")

                def f_turn():
                    e_dve.wait(pe, cf, "xr1")
                    f_act.wait(pe, cf - 1, f"relu{MT - 1}")
                    for q in range(KM):
                        for b in range(TB):
                            mm = pe.transpose(FB[:, q * CH + b * P:q * CH + (b + 1) * P],
                                              xin[:, b, q * P:(q + 1) * P], ident)
                    f_pe.done(mm, "tr")

                turned = xT if on["S"] else x2T

                def f_in(r):
                    f_act.wait(pe, cf, "xT" if r == 0 else f"e{r - 1}")
                    for m in range(2):
                        for q in range(KM):
                            c0 = (2 * r + m) * P
                            mm = pe.matmul(FB[:, m * CH:(m + 1) * CH], Win[:, q, c0:c0 + P], turned[:, q, :],
                                           start=(q == 0), stop=(q == KM - 1))
                    f_pe.done(mm, f"ip{r}")

                def f_x():
                    f_act.wait(pe, cf, "silu_x")
                    for m in range(MT):
                        mm = pe.matmul(FB[0:2 * NS + 1, 0:CH], Wx[:, m, :], xc[:, m, :],
                                       start=(m == 0), stop=(m == MT - 1))
                    f_pe.done(mm, "xp")

                def f_dt():
                    f_act.wait(pe, cf, "xd")
                    f_pe.done(pe.matmul(FB[:, CH:2 * CH], SelDt[:, :], xd[:, :], start=True, stop=True), "db")

                def p_out(b):
                    if b == 0:
                        ld_y2.wait(pe, cp)
                        p_act.wait(pe, cp - 1, "sig")
                    for m in range(MT):
                        mm = pe.matmul(PBK[:, b * DM:(b + 1) * DM], y2[:, m, b * P:(b + 1) * P], Wout[:, m, :],
                                       start=(m == 0), stop=(m == MT - 1))
                    p_pe.done(mm, f"op{b}")

                def p_turn():
                    p_dve.wait(pe, cp, "x21")
                    for q in range(KM):
                        for b in range(TB):
                            mm = pe.transpose(PBK[:, q * CH + b * P:q * CH + (b + 1) * P],
                                              rn[:, b, q * P:(q + 1) * P], ident)
                    p_pe.done(mm, "tr")

                def p_route():
                    p_act.wait(pe, cp, "x2T")
                    for b in range(TB):
                        for q in range(KM):
                            mm = pe.matmul(PBK[:, b * NE:(b + 1) * NE], x2T[:, q, b * P:(b + 1) * P], Wrt[:, q, :],
                                           start=(q == 0), stop=(q == KM - 1))
                    p_pe.done(mm, "rt")

                at = {n: [] for n in range(STEPS)}
                if on["F"]:
                    for n, r in ((1, 0), (2, 1), (3, 2), (6, 3)):
                        at[n].append(lambda r=r: f_in(r))
                    at[8].append(f_x)
                    at[9].append(f_dt)
                if on["P"]:
                    for n, f in ((4, lambda: p_out(0)), (5, lambda: p_out(1)), (10, p_turn), (11, p_route)):
                        at[n].append(f)
                if on["F"]:
                    f_turn()
                for n in range(STEPS):
                    if on["M"]:
                        gate_up(n)
                    for lag, step in ((3, turn), (4, down)):
                        if on["M"] and n >= lag:
                            step(cm_, n - lag)
                        if on["Z"] and n < lag:
                            step(cz, n - lag + STEPS)
                    if on["Y"] and n == 0:
                        add_states(i - FIRST_Y, NSIG - 1)
                    if not on["M"]:
                        for f in at[n]:
                            f()
                    if on["S"] and n and n % NBETA == 0:
                        add_states(i, n // NBETA - 1)
                    if on["M"]:
                        for f in at[n]:
                            f()

            run(pe, body)

        @block.scalar
        def _(act):
            for s in (f_act, s_act, p_act, m_in, m_th, m_uc, m_aT, m_my):
                s.credit(act)
            act.wait_ge(ld_w, 16 * len(early))
            act.activation(ADall[:, :, 0:UNITS], ADall[:, :, 0:UNITS], ACT.Exp).then_inc(w_act, 1)
            act.wait_ge(w_dve, 2)

            def body(k, on, base=0):
                i = k + base
                cf, cp, cm_, cz = i - FIRST_F, i - FIRST_P, i - FIRST_M, i - FIRST_Z

                def decay(n):
                    beta = n % NBETA
                    if n == 0:
                        s_act.wait(act, i - 1, f"dA{UNITS - 1}")
                        s_act.done(act.activation(Acur[:, :], ADall[:, i % MT, 0:UNITS], ACT.Copy), "ad")
                        s_act.wait(act, i, "ad")
                    if n < NBETA:
                        ld_dt[beta].wait(act, i)
                    s_sc.wait(act, i if n >= NA else i - 1, f"h{(n - NA) % UNITS}")
                    s_act.done(act.activation(dA[:, n % NA, :], dtr[:, beta, :], ACT.Exp, scale=Acur[:, n:n + 1]),
                               f"dA{n}")

                def tanh(n):
                    m_pe_g.wait(act, cm_, f"g{n}")
                    m_pe_t.wait(act, cm_ if n >= NTH else cm_ - 1, f"t{(n - NTH) % STEPS}")
                    m_th.done(act.activation(th[:, n % NTH, :], GU[n % 2][:, 0:2 * DE], ACT.Tanh, scale=0.5), f"th{n}")

                def up(n):
                    b, p = divmod(n, PAIRS)
                    m_pool.wait(act, cm_ if n >= NUC else cm_ - 1, f"f{(n - NUC) % STEPS}")
                    if n == 0:
                        m_in.wait(act, cm_, "cm")
                    for e in range(2):
                        c = b * NE + 2 * p + e
                        ins = act.activation(uc[:, n % NUC, e * DE:(e + 1) * DE], GU[n % 2][:, (2 + e) * DE:(3 + e) * DE],
                                             ACT.Copy, scale=cm[:, c:c + 1])
                    m_uc.done(ins, f"uc{n}")

                def evac(c, n):
                    m_pe_t.wait(act, c, f"t{n}")
                    m_pe_d.wait(act, c if n >= 2 else c - 1, f"d{(n - 2) % STEPS}")
                    m_aT.done(act.activation(aT[:, n % 2, :], TR[:, 0:2 * DE], ACT.Copy), f"aT{n}")

                def evac_y(c, b):
                    m_pe_d.wait(act, c, f"d{(b + 1) * PAIRS - 1}")
                    z_dve.wait(act, c - 1, "o1")
                    m_my.done(act.activation(my[:, b, :], MY[:, b * DM:(b + 1) * DM], ACT.Copy), f"my{b}")

                def f_xT():
                    f_pe.wait(act, cf, "tr")
                    f_pe.wait(act, cf - 1, "ip3")
                    if on["S"]:
                        f_dve.wait(act, cf - 1, "dt")
                    turned = xT if on["S"] else x2T
                    f_act.done(act.activation(turned[:, :, :], FB[:, :].rearrange("p (q t) -> p q t", q=KM), ACT.Copy), "xT")

                def f_ev(r):
                    f_pe.wait(act, cf, f"ip{r}")
                    src = FB[:, :].rearrange("p (m t) -> p m t", m=2)
                    if r < 2:
                        if r == 0:
                            f_dve.wait(act, cf - 1, "dx")
                            st_dt.wait(act, cf - 1)
                        dst = xb[:, 2 * r:2 * r + 2, HIST:HIST + CH]
                    else:
                        if r == 2:
                            f_pool.wait(act, cf - 1, "ln")
                        dst = sz[:, 2 * r - 4:2 * r - 2, :]
                    f_act.done(act.activation(dst, src, ACT.Copy), f"e{r}")

                def f_silu():
                    f_act.wait(act, cf, "e3")
                    f_act.done(act.activation(sz[:, :, :], sz[:, :, :], ACT.Silu), "silu_z")
                    f_dve.wait(act, cf, f"c3{MT - 1}")
                    f_act.done(act.activation(xc[:, :, :], xc[:, :, :], ACT.Silu), "silu_x")

                def f_xd():
                    f_pe.wait(act, cf, "xp")
                    st_xd.wait(act, cf - 1)
                    f_act.done(act.activation(xd[:, :], FB[0:2 * NS + 1, 0:CH], ACT.Copy), "xd")

                def f_sp(ms):
                    if ms[0] == 0:
                        f_pe.wait(act, cf, "db")
                        st_sz.wait(act, cf)
                        f_dve.wait(act, cf, "hist")
                    for m in ms:
                        wb = dict(scale=dt_w[:, m:m + 1], bias=dt_b[:, m:m + 1])
                        f_act.done(act.activation(sz[:, m, :], FB[:, CH:2 * CH], ACT.Abs, **wb), f"abs{m}")
                        f_act.done(act.activation(dt[:, m, :], FB[:, CH:2 * CH], ACT.Relu, **wb), f"relu{m}")

                def f_exp():
                    f_act.wait(act, cf, f"abs{MT - 1}")
                    f_act.done(act.activation(sz[:, :, :], sz[:, :, :], ACT.Exp, scale=-1.0), "exp")

                def f_ln():
                    f_dve.wait(act, cf, "lost")
                    f_act.done(act.activation(sz[:, :, :], sz[:, :, :], ACT.Ln, bias=1.0), "ln")

                def p_x2T():
                    p_pe.wait(act, cp, "tr")
                    m_in.wait(act, cp - 1, "x2m")
                    p_act.done(act.activation(x2T[:, :, :], PBK[:, :].rearrange("p (q t) -> p q t", q=KM), ACT.Copy), "x2T")

                def p_sig():
                    p_pe.wait(act, cp, "rt")
                    p_dve.wait(act, cp - 1, "comb")
                    p_act.done(act.activation(R[:, 0, :], PBK[:, 0:TB * NE], ACT.Sigmoid), "sig")

                def take_x():
                    m_pe_g.wait(act, cm_ - 1, f"g{STEPS - 1}")
                    p_act.wait(act, cm_, "x2T")
                    m_in.done(act.activation(x2m[:, :, :], x2T[:, :, :], ACT.Copy), "x2m")

                def take_c():
                    m_uc.wait(act, cm_ - 1, f"uc{STEPS - 1}")
                    p_dve.wait(act, cm_, "comb")
                    m_in.done(act.activation(cm[:, :], comb[:, :], ACT.Copy), "cm")

                for n in range(STEPS):
                    if on["M"] and n == 0:
                        take_x()
                    if on["S"]:
                        if n == 0:
                            decay(0)
                        if n + 1 < UNITS:
                            decay(n + 1)
                    if on["M"]:
                        tanh(n)
                        if n == 0:
                            take_c()
                        up(n)
                        if n >= 3:
                            evac(cm_, n - 3)
                        if n == PAIRS + 3:
                            evac_y(cm_, 0)
                    if on["Z"]:
                        if n < 3:
                            evac(cz, n - 3 + STEPS)
                        if n == 3:
                            evac_y(cz, 1)
                    if on["P"]:
                        if n == 10:
                            p_x2T()
                        if n == 11:
                            p_sig()
                    if on["F"]:
                        if n == 0:
                            f_xT()
                        for m, r in ((1, 0), (2, 1), (3, 2), (6, 3)):
                            if n == m:
                                f_ev(r)
                        if n == 7:
                            f_silu()
                        if n == 8:
                            f_xd()
                        if n == 9:
                            f_sp(range(0, 2))
                        if n == 10:
                            f_sp(range(2, MT))
                            f_exp()
                        if n == 11:
                            f_ln()

            run(act, body)

        @block.gpsimd
        def _(pool):
            for s in (s_up, s_hc, y_pool, f_pool, m_pool):
                s.credit(pool)

            def body(k, on, base=0):
                i = k + base
                cf, cm_ = i - FIRST_F, i - FIRST_M

                def weigh(n):
                    m_uc.wait(pool, cm_, f"uc{n}")
                    m_dve.wait(pool, cm_, f"a{n}")
                    m_pool.done(pool.tensor_tensor(th[:, n % NTH, :], th[:, n % NTH, :], uc[:, n % NUC, :], ALU.mult), f"f{n}")

                def inputs(n):
                    s, beta = divmod(n, NBETA)
                    if s == 0:
                        ld_dt[beta].wait(pool, i)
                    ld_bc[s].wait(pool, i // NCH)
                    back, m = user_before(SLOT, n)
                    s_pe.wait(pool, i + back, f"y{m // NBETA}")
                    s_up.done(pool.tensor_tensor(hs[:, SLOT[n], :], dxr[:, beta, :], Bb[:, s, :], ALU.mult), f"u{n}")

                for n in range(UNITS):
                    group_ends = n % NBETA == NBETA - 1
                    if on["M"] and n >= 1 and not group_ends:
                        weigh(n - 1)
                    if on["S"]:
                        for m in range(0 if n == 0 else n + 2, min(n + 3, UNITS)):
                            if m in POOL_UNITS:
                                inputs(m)
                    if on["F"] and n == 12:
                        f_act.wait(pool, cf, "ln")
                        f_pool.done(pool.tensor_tensor(low, low, sz[:, :, :], ALU.add), "ln")
                    if on["Y"] and n == 2:
                        y_dve.wait(pool, i - FIRST_Y, "skip1")
                        ld_gt.wait(pool, i - FIRST_Y)
                        y_pool.done(pool.tensor_tensor(yt[:, :], yt[:, :], gt, ALU.mult), "gate")
                    if on["S"]:
                        s_sc.wait(pool, i, f"h{n}")
                        if n % NBETA == 0:
                            ld_bc[n // NBETA].wait(pool, i // NCH)
                        h = hs[:, SLOT[n], :]
                        s_hc.done(pool.tensor_tensor(h, h, Cb[:, n // NBETA, :], ALU.mult), f"c{n}")
                    if on["M"] and n >= 1 and group_ends:
                        weigh(n - 1)
                if on["M"]:
                    weigh(STEPS - 1)

            run(pool, body)

        @block.vector
        def _(dve):
            for s in (e_dve, f_dve, s_u, s_sc, y_dve, p_dve, m_dve, z_dve):
                s.credit(dve)
            dve.wait_ge(ld_w, 16 * len(early))
            for q in range(KM):
                ins = dve.tensor_scalar(Win[:, q, :], Win[:, q, :], norm_w[:, q:q + 1], None, ALU.mult)
            ins.then_inc(w_dve, 1)
            dve.wait_ge(w_act, 1)
            dve.tensor_scalar(ADall[:, :, 0:UNITS], ADall[:, :, 0:UNITS], -1.0, None, ALU.mult).then_inc(w_dve, 1)
            dve.memset(xb[:, :, :], 0.0).then_inc(w_dve, 1)
            dve.wait_ge(w_dve, 3)

            def body(k, on, base=0):
                i = k + base
                ce, cf, cp, cm_, cz, iy = i - FIRST_E, i - FIRST_F, i - FIRST_P, i - FIRST_M, i - FIRST_Z, i - FIRST_Y

                def op(steps, it, name, emit, *after):
                    for a in after[-1:]:
                        steps.wait(dve, it, a)
                    steps.done(emit(), name)

                def rsqrt(steps, it, tag, w, after):
                    v, y, a = w[:, 0, :], w[:, 1, :], w[:, 2, :]
                    op(steps, it, f"{tag}_half", lambda: dve.tensor_scalar(
                        a.bitcast(I32), v.bitcast(I32), 1, None, ALU.logical_shift_right), after)
                    yield
                    op(steps, it, f"{tag}_guess", lambda: dve.tensor_scalar(
                        y.bitcast(I32), a.bitcast(I32), -1.0, RSQRT_MAGIC, ALU.mult, ALU.add), f"{tag}_half")
                    yield
                    last = f"{tag}_guess"
                    for n in range(3):
                        op(steps, it, f"{tag}_a{n}", lambda: dve.scalar_tensor_tensor(
                            out=a, in0=y, scalar=-0.5, in1=y, op0=ALU.mult, op1=ALU.mult), last)
                        yield
                        op(steps, it, f"{tag}_b{n}", lambda: dve.tensor_tensor(a, a, v, ALU.mult), f"{tag}_a{n}")
                        yield
                        op(steps, it, f"{tag}_y{n}", lambda: dve.scalar_tensor_tensor(
                            out=y, in0=a, scalar=1.5, in1=y, op0=ALU.add, op1=ALU.mult), f"{tag}_b{n}")
                        last = f"{tag}_y{n}"
                        yield

                def stats(steps, it, pre, src, st, mv, after):
                    for b in range(TB):
                        op(steps, it, f"{pre}bn{b}", lambda: dve.bn_stats(st[:, b, :], src[:, b, :]), *after)
                        yield
                    op(steps, it, f"{pre}both", lambda: dve.memset(mark[:, :], 0.0), f"{pre}bn1")
                    for b in range(TB):
                        op(steps, it, f"{pre}ag{b}", lambda: dve.bn_aggr(mv[:, b, :], st[:, b, :]))
                        yield

                def part_e():
                    ld_xin.wait(dve, ce)
                    yield from stats(e_dve, ce, "", xin, f_st, f_mv, ())
                    op(e_dve, ce, "w1", lambda: dve.tensor_scalar(f_w[:, 0, 0:TB], f_mv[:, :, 1], LN_EPS, None, ALU.add), "ag1")
                    yield
                    op(e_dve, ce, "w2", lambda: dve.tensor_scalar(
                        f_w[:, 0, TB:2 * TB], f_mv[:, :, 1], 1.0 + RMS_EPS, LN_EPS * RMS_EPS, ALU.mult, ALU.add))
                    yield
                    yield from rsqrt(e_dve, ce, "r", f_w, "w2")
                    for k, (name, src) in enumerate((("mean", f_mv[:, :, 0]), ("dev", f_w[:, 1, 0:TB]))):
                        op(e_dve, ce, name, lambda: dve.tensor_scalar(
                            ln1[:, ce, k * TB:(k + 1) * TB], src, 1.0, None, ALU.mult), "r_y2")
                        yield
                    for b in range(TB):
                        op(e_dve, ce, f"xr{b}", lambda: dve.tensor_scalar(
                            xin[:, b, :], xin[:, b, :], f_mv[:, b, 0:1], f_w[:, 1, TB + b:TB + b + 1],
                            ALU.subtract, ALU.mult))
                        yield

                def part_f2():
                    st_dx.wait(dve, cf - 1)
                    f_act.wait(dve, cf, "e1")
                    for t in range(TAPS):
                        for m in range(MT):
                            src = xb[:, m, t:t + CH]
                            if t == 0:
                                op(f_dve, cf, f"c{t}{m}", lambda: dve.tensor_scalar(
                                    xc[:, m, :], src, conv_w[:, m, t:t + 1], conv_b[:, m:m + 1], ALU.mult, ALU.add))
                            else:
                                op(f_dve, cf, f"c{t}{m}", lambda: dve.scalar_tensor_tensor(
                                    out=xc[:, m, :], in0=src, scalar=conv_w[:, m, t:t + 1], in1=xc[:, m, :],
                                    op0=ALU.mult, op1=ALU.add), f"c{t - 1}{m}")
                            yield
                    ld_kp.wait(dve, cf)
                    op(f_dve, cf, "hist", lambda: dve.tensor_scalar(
                        xb[:, :, 0:HIST], xb[:, :, CH:CH + HIST], kp[:, 0:1], None, ALU.mult))
                    yield

                def part_f3():
                    f_act.wait(dve, cf, "exp")
                    if on["P"]:
                        st_x1.wait(dve, cp)
                        p_dve.wait(dve, cp, "x21")
                    op(f_dve, cf, "near", lambda: dve.tensor_scalar(low, sz[:, :, :], 1.0, -1.0, ALU.add, ALU.add))
                    yield
                    op(f_dve, cf, "lost", lambda: dve.tensor_tensor(low, sz[:, :, :], low, ALU.subtract), "near")
                    yield

                def part_f4():
                    f_pool.wait(dve, cf, "ln")
                    op(f_dve, cf, "dt", lambda: dve.tensor_tensor(dt, dt, low, ALU.add))
                    yield
                    st_xc.wait(dve, cf)
                    f_pe.wait(dve, cf, "xp")
                    op(f_dve, cf, "dx", lambda: dve.tensor_tensor(xc[:, :, :], dt, xc[:, :, :], ALU.mult), "dt")
                    yield

                def inputs(n):
                    s, beta = divmod(n, NBETA)
                    if s == 0:
                        ld_dt[beta].wait(dve, i)
                    if beta == 0:
                        ld_bc[s].wait(dve, i // NCH)
                    back, m = user_before(SLOT, n)
                    s_pe.wait(dve, i + back, f"y{m // NBETA}")
                    s_u.done(dve.tensor_tensor(hs[:, SLOT[n], :], dxr[:, beta, :], Bb[:, s, :], ALU.mult), f"u{n}")

                def scan(n):
                    s_act.wait(dve, i, f"dA{n}")
                    of_u(n).wait(dve, i, f"u{n}")
                    s_sc.done(dve.tensor_tensor_scan(hs[:, SLOT[n], :], dA[:, n % NA, :], hs[:, SLOT[n], :], 0.0,
                                                     ALU.mult, ALU.add), f"h{n}")

                def part_y():
                    s_pe.wait(dve, iy, f"y{NSIG - 1}")
                    ld_yt.wait(dve, iy)
                    for h in range(2):
                        op(y_dve, iy, f"skip{h}", lambda: dve.scalar_tensor_tensor(
                            out=yt[:, h * 512:(h + 1) * 512], in0=yt[:, h * 512:(h + 1) * 512],
                            scalar=ADall[:, iy % MT, UNITS:UNITS + 1], in1=Y[h][:, :], op0=ALU.mult, op1=ALU.add))
                        yield

                def part_p():
                    ld_p.wait(dve, cp)
                    for b in range(TB):
                        op(p_dve, cp, f"xn{b}", lambda: dve.tensor_scalar(
                            rn[:, b, :], x1[:, b, :], ln1[:, cp, b:b + 1], ln1[:, cp, TB + b:TB + b + 1],
                            ALU.subtract, ALU.mult))
                        yield
                    p_pe.wait(dve, cp, f"op{TB - 1}")
                    op(p_dve, cp, "r", lambda: dve.tensor_tensor(
                        rn[:, :, :], PBK[:, :].rearrange("p (b h) -> p b h", b=TB), rn[:, :, :], ALU.add), "xn1")
                    yield
                    yield from stats(p_dve, cp, "", rn, p_st, p_mv, ("r",))
                    op(p_dve, cp, "w1", lambda: dve.tensor_scalar(p_w[:, 0, :], p_mv[:, :, 1], LN_EPS, None, ALU.add), "ag1")
                    yield
                    yield from rsqrt(p_dve, cp, "r", p_w, "w1")
                    for b in range(TB):
                        op(p_dve, cp, f"o{b}", lambda: dve.tensor_scalar(
                            rn[:, b, :], rn[:, b, :], p_mv[:, b, 0:1], p_w[:, 1, b:b + 1], ALU.subtract, ALU.mult), "r_y2")
                        yield
                    op(p_dve, cp, "x1", lambda: dve.tensor_tensor(x1, rn[:, :, :], x1, ALU.add), "o1")
                    yield
                    yield from stats(p_dve, cp, "B", x1, p_st, p_mv, ("x1",))
                    op(p_dve, cp, "Bw1", lambda: dve.tensor_scalar(p_w[:, 0, :], p_mv[:, :, 1], LN_EPS, None, ALU.add), "Bag1")
                    yield
                    yield from rsqrt(p_dve, cp, "q", p_w, "Bw1")
                    for b in range(TB):
                        op(p_dve, cp, f"x2{b}", lambda: dve.tensor_scalar(
                            rn[:, b, :], x1[:, b, :], p_mv[:, b, 0:1], p_w[:, 1, b:b + 1], ALU.subtract, ALU.mult), "q_y2")
                        yield

                def part_p2():
                    p_act.wait(dve, cp, "sig")
                    G = TB * NG
                    score, sfc, tmp, w = (R[:, k, :] for k in (0, 1, 2, 3))
                    q4 = sfc.rearrange("p (g e) -> p g e", e=NE // NG)
                    hi, lo = (R[:, k, 0:2 * G].rearrange("p (g e) -> p g e", e=2) for k in (4, 5))
                    top1, ta, tb, gs, gr = (R[:, 6, k * G:(k + 1) * G] for k in (0, 1, 2, 3, 1))
                    gm = R[:, 7, 0:G]
                    rk = R[:, 8, :]
                    ws, wr = R[:, 9, 0:TB], R[:, 9, TB:2 * TB]
                    gg, ge = (R[:, k, :].rearrange("p (b i j) -> p b i j", b=TB, i=NG) for k in (10, 11))
                    tt = dve.tensor_tensor
                    o = lambda name, emit, *after: op(p_dve, cp, name, emit, *after)
                    o("sfc", lambda: tt(sfc, score, Ebias[:, :], ALU.add)); yield
                    o("hi", lambda: tt(hi, q4[:, :, 0:2], q4[:, :, 2:4], ALU.max), "sfc"); yield
                    o("lo", lambda: tt(lo, q4[:, :, 0:2], q4[:, :, 2:4], ALU.min)); yield
                    o("t1", lambda: tt(top1, hi[:, :, 0], hi[:, :, 1], ALU.max), "lo"); yield
                    o("t2a", lambda: tt(ta, hi[:, :, 0], hi[:, :, 1], ALU.min)); yield
                    o("t2b", lambda: tt(tb, lo[:, :, 0], lo[:, :, 1], ALU.max)); yield
                    o("t2", lambda: tt(tb, ta, tb, ALU.max), "t2b"); yield
                    o("gs", lambda: tt(gs, top1, tb, ALU.add), "t2"); yield
                    gv = gs.rearrange("p (b g) -> p b g", b=TB)
                    g_j = gv.unsqueeze(2).broadcast_to([P, TB, NG, NG])
                    g_i = gv.unsqueeze(3).broadcast_to([P, TB, NG, NG])
                    bg = before_g.rearrange("p (i j) -> p i j", i=NG).unsqueeze(1).broadcast_to([P, TB, NG, NG])
                    o("ggt", lambda: tt(gg, g_j, g_i, ALU.is_gt), "gs"); yield
                    o("geq", lambda: tt(ge, g_j, g_i, ALU.is_equal)); yield
                    o("gq", lambda: tt(ge, ge, bg, ALU.mult), "geq"); yield
                    o("ga", lambda: tt(gg, gg, ge, ALU.add), "gq"); yield
                    o("gr", lambda: dve.tensor_reduce(gr, R[:, 10, :].rearrange("p (g j) -> p g j", j=NG), AX.X, ALU.add), "ga"); yield
                    o("gm", lambda: dve.tensor_scalar(gm, gr, float(TOPG), None, ALU.is_lt), "gr"); yield
                    t4 = tmp.rearrange("p (g e) -> p g e", e=NE // NG)
                    o("tmp", lambda: tt(t4, q4, gm.unsqueeze(2).broadcast_to([P, G, NE // NG]), ALU.mult), "gm"); yield
                    tv = tmp.rearrange("p (b e) -> p b e", b=TB)
                    e_j = tv.unsqueeze(2).broadcast_to([P, TB, NE, NE])
                    e_i = tv.unsqueeze(3).broadcast_to([P, TB, NE, NE])
                    gt_, eq_ = (RR[:, k, :].rearrange("p (b i j) -> p b i j", b=TB, i=NE) for k in (0, 1))
                    be = before.rearrange("p (i j) -> p i j", i=NE).unsqueeze(1).broadcast_to([P, TB, NE, NE])
                    o("gt", lambda: tt(gt_, e_j, e_i, ALU.is_gt), "tmp"); yield
                    o("eq", lambda: tt(eq_, e_j, e_i, ALU.is_equal)); yield
                    o("eqb", lambda: tt(eq_, eq_, be, ALU.mult), "eq"); yield
                    o("ad", lambda: tt(RR[:, 0, :], RR[:, 0, :], RR[:, 1, :], ALU.add), "eqb"); yield
                    o("rk", lambda: dve.tensor_reduce(rk, RR[:, 0, :].rearrange("p (r j) -> p r j", j=NE), AX.X, ALU.add), "ad"); yield
                    o("w", lambda: dve.scalar_tensor_tensor(out=w, in0=rk, scalar=float(TOPK), in1=score,
                                                            op0=ALU.is_lt, op1=ALU.mult), "rk"); yield
                    wv = w.rearrange("p (b e) -> p b e", b=TB)
                    o("ws", lambda: dve.tensor_reduce(ws, wv, AX.X, ALU.add), "w"); yield
                    o("we", lambda: dve.tensor_scalar(ws, ws, 1e-20, None, ALU.add), "ws"); yield
                    o("wr", lambda: dve.reciprocal(wr, ws), "we"); yield
                    m_in.wait(dve, cp - 1, "cm")
                    op(p_dve, cp, "comb", lambda: dve.scalar_tensor_tensor(
                        out=comb[:, :].rearrange("p (b e) -> p b e", b=TB), in0=wv, scalar=0.5,
                        in1=wr.unsqueeze(2).broadcast_to([P, TB, NE]), op0=ALU.mult, op1=ALU.mult), "wr")
                    yield

                def expert(n):
                    m_th.wait(dve, cm_, f"th{n}")
                    m_uc.wait(dve, cm_, f"uc{n}")
                    op(m_dve, cm_, f"a{n}", lambda: dve.scalar_tensor_tensor(
                        out=th[:, n % NTH, :], in0=th[:, n % NTH, :], scalar=1.0, in1=GU[n % 2][:, 0:2 * DE],
                        op0=ALU.add, op1=ALU.mult))
                    yield

                def part_z():
                    m_my.wait(dve, cz, f"my{TB - 1}")
                    ld_x1.wait(dve, cz)
                    yield from stats(z_dve, cz, "", my, z_st, z_mv, ())
                    op(z_dve, cz, "w1", lambda: dve.tensor_scalar(z_w[:, 0, :], z_mv[:, :, 1], LN_EPS, None, ALU.add), "ag1")
                    yield
                    yield from rsqrt(z_dve, cz, "r", z_w, "w1")
                    for b in range(TB):
                        op(z_dve, cz, f"o{b}", lambda: dve.tensor_scalar(
                            my[:, b, :], my[:, b, :], z_mv[:, b, 0:1], z_w[:, 1, b:b + 1], ALU.subtract, ALU.mult), "r_y2")
                        yield
                    op(z_dve, cz, "out", lambda: dve.tensor_tensor(x1m[:, :, :], my[:, :, :], x1m[:, :, :], ALU.add), "o1")
                    yield

                chains = dict(E1=part_e(), F2=part_f2(), F3=part_f3(), F4=part_f4(), P1=part_p(), P2=part_p2(), Z=part_z(), Y=part_y())

                def shuffle(n):
                    left = {c: k for c, k in PLAN.get(n, {}).items() if on[c[0]]}
                    while left:
                        for c in list(left):
                            if next(chains[c], "end") == "end":
                                del left[c]
                                continue
                            yield
                            left[c] -= 1
                            if not left[c]:
                                del left[c]

                def big(n):
                    if on["S"]:
                        ahead = [m for m in range(0 if n == 0 else n + 1, min(n + 2, UNITS)) if m not in POOL_UNITS]
                        if n == 0:
                            inputs(ahead.pop(0))
                            yield
                        scan(n)
                        yield
                        for m in ahead:
                            inputs(m)
                            yield
                    if on["M"]:
                        yield from expert(n)

                for n in range(UNITS):
                    small, want = shuffle(n), sum(min(k, 10) for c, k in PLAN.get(n, {}).items() if on[c[0]])
                    slots = (2 if on["S"] else 0) + (1 if on["M"] else 0)
                    each = -(-want // slots) if slots else 0
                    for _ in big(n):
                        for _ in range(each):
                            next(small, None)
                    for _ in small:
                        pass

            run(dve, body)


def kernel(**inputs):
    import concourse.bacc as bacc
    from concourse.bass_utils import run_bass_kernel_spmd

    g = {k.removeprefix("L0_"): np.asarray(v) for k, v in inputs.items()}
    tiles = lambda a: np.ascontiguousarray(a.reshape(-1, P, *a.shape[1:]).swapaxes(0, 1))
    eye = np.eye(P, dtype=np.float32)
    order = list(range(1, 2 * NS + 1)) + [0]
    gate = g["ffn_gate_proj"].transpose(2, 0, 1).reshape(DM, PAIRS, 2 * DE)
    up = g["ffn_up_proj"].transpose(2, 0, 1).reshape(DM, PAIRS, 2 * DE)
    alog = g["attn_A_log"].reshape(MT, NBETA, CB, NSIG, SG).transpose(4, 2, 0, 3, 1).reshape(P, MT, UNITS)
    col = lambda a: tiles(a.reshape(DI, 1))[:, :, 0]
    conv = tiles(g["attn_conv_w"].reshape(DI, TAPS)).reshape(P, MT * TAPS)
    i_, j_ = np.arange(NE), np.arange(NG)
    before = (i_[None, :] < i_[:, None]).astype(np.float32).reshape(1, -1)
    before_g = (j_[None, :] < j_[:, None]).astype(np.float32).reshape(1, -1)
    sel_dt = np.zeros((2 * NS + 1, P), np.float32)
    sel_dt[2 * NS] = 1.0
    keep = np.ones((NCH, P, 1), np.float32)
    keep[NCH - 1] = 0.0
    arrays = dict(
        x=np.ascontiguousarray(g["attn_x"].reshape(BATCH * SEQ, DM)),
        w_in=tiles(g["attn_in_proj_w"]),
        w_out=tiles(g["attn_out_proj_w"]),
        w_gu=tiles(np.concatenate([gate, up], axis=2)),
        w_dn=np.ascontiguousarray(g["ffn_down_proj"].transpose(2, 0, 1)),
        w_x=tiles(g["attn_x_proj_w"][:, order]),
        w_rt=tiles(np.ascontiguousarray(g["ffn_gate_weight"].T)),
        cols=np.concatenate([conv, col(g["attn_conv_b"]), col(g["attn_dt_proj_w"]), col(g["attn_dt_proj_b"]),
                             col(g["attn_D"]), tiles(g["attn_norm_w"].reshape(DM, 1))[:, :, 0]], axis=1),
        alog=np.concatenate([alog, col(g["attn_D"])[:, :, None]], axis=2),
        ebias=np.broadcast_to(np.tile(g["ffn_e_bias"], TB), (P, TB * NE)),
        consts=np.concatenate([eye, np.tile(np.eye(CB, dtype=np.float32), (SG, 1)),
                               np.broadcast_to(before, (P, NE * NE)), np.broadcast_to(before_g, (P, NG * NG))], axis=1),
        sel_dt=sel_dt,
        keep=keep,
    )
    nc = bacc.Bacc("TRN2", target_bir_lowering=False, num_devices=1)
    feed, args = {}, []
    for name, a in arrays.items():
        a = np.ascontiguousarray(a)
        feed[f"in_{name}"] = a
        args.append(nc.dram_tensor(f"in_{name}", a.shape, mybir.dt.from_np(a.dtype), kind="ExternalInput").ap())
    o = nc.dram_tensor("out_0", (BATCH * SEQ, DM), F32, kind="ExternalOutput").ap()
    sandwich_kernel(nc, *args, o)
    r = run_bass_kernel_spmd(nc, [feed], core_ids=[0])
    return r.results[0]["out_0"].reshape(BATCH, SEQ, DM)
```
